# Optimizing a Trainium2 kernel written in Bass

```python
import numpy as np
import jax
import jax.numpy as jnp

def _softmax(x, axis=-1):
    return jax.nn.softmax(x, axis=axis)

def _gelu(x):
    return jax.nn.gelu(x, approximate=True)

def _silu(x):
    return jax.nn.silu(x)

def _sigmoid(x):
    return jax.nn.sigmoid(x)

def _layernorm(x, axis=-1, eps=1e-05):
    m = jnp.mean(x, axis=axis, keepdims=True)
    v = jnp.var(x, axis=axis, keepdims=True)
    return (x - m) / jnp.sqrt(v + eps)

def _scatter_add(tgt, idx, src, axis=0):
    return tgt.at[idx].add(src)

def _segment_sum(src, seg, n):
    return jax.ops.segment_sum(src, seg, n)
kernel_name = 'mk_seq_postln_d1_jaxref_r4_43dfb8'

def setup_inputs(seed: int=0):
    np.random.seed(seed)
    _w = jnp.asarray

    def _L0_attn_setup():
        import jax, jax.numpy as jnp
        import numpy as np
        B, S, D = (4, 512, 256)
        H, C = (16, 64)
        HID = H * C
        key = jax.random.key(seed)
        ks = jax.random.split(key, 9)
        scale = 0.02
        return {'x': jax.random.normal(ks[0], (B, S, D), dtype=jnp.float32), 'Wq': jax.random.normal(ks[1], (D, HID), dtype=jnp.float32) * scale, 'bq': jnp.zeros((HID,), dtype=jnp.float32), 'Wk': jax.random.normal(ks[2], (D, HID), dtype=jnp.float32) * scale, 'bk': jnp.zeros((HID,), dtype=jnp.float32), 'Wv': jax.random.normal(ks[3], (D, HID), dtype=jnp.float32) * scale, 'bv': jnp.zeros((HID,), dtype=jnp.float32), 'Wo': jax.random.normal(ks[4], (HID, D), dtype=jnp.float32) * scale, 'bo': jnp.zeros((D,), dtype=jnp.float32)}
    _L0_attn_in = _L0_attn_setup()

    def _L0_ffn_setup():
        import jax, jax.numpy as jnp
        import numpy as np
        D = 256
        H = 4
        HD = D // H
        E = 8
        FF = 1024
        CAP_FACTOR = 1.0

        def _ln(x, g, b, eps=1e-05):
            mu = jnp.mean(x, -1, keepdims=True)
            v = jnp.mean((x - mu) ** 2, -1, keepdims=True)
            return (x - mu) * jax.lax.rsqrt(v + eps) * g + b

        def _mha(x, w, b, ow, ob):
            L, N, _ = x.shape
            qkv = x @ w.T + b
            q, k, v = jnp.split(qkv, 3, axis=-1)
            rh = lambda t: t.reshape(L, N, H, HD).transpose(1, 2, 0, 3)
            q, k, v = (rh(q), rh(k), rh(v))
            scores = jnp.einsum('nhld,nhmd->nhlm', q, k) / np.float32(np.sqrt(HD))
            attn = jax.nn.softmax(scores, axis=-1)
            o = jnp.einsum('nhlm,nhmd->nhld', attn, v).transpose(2, 0, 1, 3).reshape(L, N, D)
            return o @ ow.T + ob

        def _moe(x, wg, w1, b1, w2, b2):
            L, N, _ = x.shape
            S = L * N
            cap = int(CAP_FACTOR * S) // E
            xf = x.reshape(S, D)
            gates = jax.nn.softmax(xf @ wg, axis=-1)
            idx = jnp.argmax(gates, axis=-1)
            mask1 = jax.nn.one_hot(idx, E, dtype=x.dtype)
            loc = jnp.sum((jnp.cumsum(mask1, 0) - 1.0) * mask1, -1).astype(jnp.int32)
            keep = loc < cap
            gate_val = jnp.take_along_axis(gates, idx[:, None], -1)[:, 0]
            slot = jnp.where(keep, idx.astype(jnp.int32) * cap + loc, E * cap)
            disp = jnp.zeros((E * cap, D), x.dtype).at[slot].set(xf, mode='drop')
            disp = disp.reshape(E, cap, D)
            h = jnp.einsum('ecd,edf->ecf', disp, w1) + b1[:, None, :]
            y = (jnp.einsum('ecf,efd->ecd', h, w2) + b2[:, None, :]).reshape(E * cap, D)
            out = jnp.where(keep[:, None], gate_val[:, None] * y[jnp.minimum(slot, E * cap - 1)], 0.0)
            return out.reshape(L, N, D)
        key = jax.random.key(seed)
        ks = jax.random.split(key, 8)
        L, N = (256, 16)
        s = 0.02
        return {'x': jax.random.normal(ks[0], (L, N, D), jnp.float32), 'in_proj_w': jax.random.normal(ks[1], (3 * D, D), jnp.float32) * s, 'in_proj_b': jnp.zeros((3 * D,), jnp.float32), 'out_proj_w': jax.random.normal(ks[2], (D, D), jnp.float32) * s, 'out_proj_b': jnp.zeros((D,), jnp.float32), 'ln1_g': jnp.ones((D,), jnp.float32), 'ln1_b': jnp.zeros((D,), jnp.float32), 'ln2_g': jnp.ones((D,), jnp.float32), 'ln2_b': jnp.zeros((D,), jnp.float32), 'wg': jax.random.normal(ks[3], (D, E), jnp.float32) * s, 'w1': jax.random.normal(ks[4], (E, D, FF), jnp.float32) * s, 'b1': jnp.zeros((E, FF), jnp.float32), 'w2': jax.random.normal(ks[5], (E, FF, D), jnp.float32) * s, 'b2': jnp.zeros((E, D), jnp.float32)}
    _L0_ffn_in = _L0_ffn_setup()
    _d = {'L0_attn_x': _L0_attn_in['x'], 'L0_attn_Wq': _L0_attn_in['Wq'], 'L0_attn_bq': _L0_attn_in['bq'], 'L0_attn_Wk': _L0_attn_in['Wk'], 'L0_attn_bk': _L0_attn_in['bk'], 'L0_attn_Wv': _L0_attn_in['Wv'], 'L0_attn_bv': _L0_attn_in['bv'], 'L0_attn_Wo': _L0_attn_in['Wo'], 'L0_attn_bo': _L0_attn_in['bo'], 'L0_ffn_in_proj_w': _L0_ffn_in['in_proj_w'], 'L0_ffn_in_proj_b': _L0_ffn_in['in_proj_b'], 'L0_ffn_out_proj_w': _L0_ffn_in['out_proj_w'], 'L0_ffn_out_proj_b': _L0_ffn_in['out_proj_b'], 'L0_ffn_ln1_g': _L0_ffn_in['ln1_g'], 'L0_ffn_ln1_b': _L0_ffn_in['ln1_b'], 'L0_ffn_ln2_g': _L0_ffn_in['ln2_g'], 'L0_ffn_ln2_b': _L0_ffn_in['ln2_b'], 'L0_ffn_wg': _L0_ffn_in['wg'], 'L0_ffn_w1': _L0_ffn_in['w1'], 'L0_ffn_b1': _L0_ffn_in['b1'], 'L0_ffn_w2': _L0_ffn_in['w2'], 'L0_ffn_b2': _L0_ffn_in['b2']}
    _x0 = _d['L0_attn_x']
    _d['L0_attn_x'] = jax.random.normal(jax.random.fold_in(jax.random.key(seed), 1), (8, 1024, 256), dtype=_x0.dtype)
    del _x0
    return _d

def reference(L0_attn_x, L0_attn_Wq, L0_attn_bq, L0_attn_Wk, L0_attn_bk, L0_attn_Wv, L0_attn_bv, L0_attn_Wo, L0_attn_bo, L0_ffn_in_proj_w, L0_ffn_in_proj_b, L0_ffn_out_proj_w, L0_ffn_out_proj_b, L0_ffn_ln1_g, L0_ffn_ln1_b, L0_ffn_ln2_g, L0_ffn_ln2_b, L0_ffn_wg, L0_ffn_w1, L0_ffn_b1, L0_ffn_w2, L0_ffn_b2):

    def _L0_attn_ref(x, Wq, bq, Wk, bk, Wv, bv, Wo, bo):
        import jax, jax.numpy as jnp
        import numpy as np
        B, S, D = (4, 512, 256)
        H, C = (16, 64)
        HID = H * C
        b, s, _ = x.shape
        inv_sqrt_c = jnp.asarray(1.0 / C ** 0.5, dtype=x.dtype)
        Q = (x @ Wq + bq).reshape(b, s, H, C) * inv_sqrt_c
        K = (x @ Wk + bk).reshape(b, s, H, C)
        V = (x @ Wv + bv).reshape(b, s, H, C)
        scores = jnp.einsum('bshq,bshk->bshqk', Q, K)
        mask = jnp.triu(jnp.ones((C, C), dtype=bool), 1)
        scores = jnp.where(mask, jnp.asarray(-jnp.inf, scores.dtype), scores)
        w = jax.nn.softmax(scores, axis=-1)
        attn = jnp.einsum('bshqk,bshk->bshq', w, V)
        attn = attn.reshape(b, s, HID)
        return attn @ Wo + bo

    def _L0_ffn_ref(x, in_proj_w, in_proj_b, out_proj_w, out_proj_b, ln1_g, ln1_b, ln2_g, ln2_b, wg, w1, b1, w2, b2):
        import jax, jax.numpy as jnp
        import numpy as np
        D = 256
        H = 4
        HD = D // H
        E = 8
        FF = 1024
        CAP_FACTOR = 1.0

        def _ln(x, g, b, eps=1e-05):
            mu = jnp.mean(x, -1, keepdims=True)
            v = jnp.mean((x - mu) ** 2, -1, keepdims=True)
            return (x - mu) * jax.lax.rsqrt(v + eps) * g + b

        def _mha(x, w, b, ow, ob):
            L, N, _ = x.shape
            qkv = x @ w.T + b
            q, k, v = jnp.split(qkv, 3, axis=-1)
            rh = lambda t: t.reshape(L, N, H, HD).transpose(1, 2, 0, 3)
            q, k, v = (rh(q), rh(k), rh(v))
            scores = jnp.einsum('nhld,nhmd->nhlm', q, k) / np.float32(np.sqrt(HD))
            attn = jax.nn.softmax(scores, axis=-1)
            o = jnp.einsum('nhlm,nhmd->nhld', attn, v).transpose(2, 0, 1, 3).reshape(L, N, D)
            return o @ ow.T + ob

        def _moe(x, wg, w1, b1, w2, b2):
            L, N, _ = x.shape
            S = L * N
            cap = int(CAP_FACTOR * S) // E
            xf = x.reshape(S, D)
            gates = jax.nn.softmax(xf @ wg, axis=-1)
            idx = jnp.argmax(gates, axis=-1)
            mask1 = jax.nn.one_hot(idx, E, dtype=x.dtype)
            loc = jnp.sum((jnp.cumsum(mask1, 0) - 1.0) * mask1, -1).astype(jnp.int32)
            keep = loc < cap
            gate_val = jnp.take_along_axis(gates, idx[:, None], -1)[:, 0]
            slot = jnp.where(keep, idx.astype(jnp.int32) * cap + loc, E * cap)
            disp = jnp.zeros((E * cap, D), x.dtype).at[slot].set(xf, mode='drop')
            disp = disp.reshape(E, cap, D)
            h = jnp.einsum('ecd,edf->ecf', disp, w1) + b1[:, None, :]
            y = (jnp.einsum('ecf,efd->ecd', h, w2) + b2[:, None, :]).reshape(E * cap, D)
            out = jnp.where(keep[:, None], gate_val[:, None] * y[jnp.minimum(slot, E * cap - 1)], 0.0)
            return out.reshape(L, N, D)
        y1 = _ln(x + _mha(x, in_proj_w, in_proj_b, out_proj_w, out_proj_b), ln1_g, ln1_b)
        y2 = _ln(y1 + _moe(y1, wg, w1, b1, w2, b2), ln2_g, ln2_b)
        return y2
    x = L0_attn_x
    x = _layernorm(x + _L0_attn_ref(x, L0_attn_Wq, L0_attn_bq, L0_attn_Wk, L0_attn_bk, L0_attn_Wv, L0_attn_bv, L0_attn_Wo, L0_attn_bo), axis=-1)
    x = _layernorm(x + _L0_ffn_ref(x, L0_ffn_in_proj_w, L0_ffn_in_proj_b, L0_ffn_out_proj_w, L0_ffn_out_proj_b, L0_ffn_ln1_g, L0_ffn_ln1_b, L0_ffn_ln2_g, L0_ffn_ln2_b, L0_ffn_wg, L0_ffn_w1, L0_ffn_b1, L0_ffn_w2, L0_ffn_b2), axis=-1)
    return x

_drawn_inputs = setup_inputs


def setup_inputs(seed=0):
    import zlib

    import numpy as np

    out = dict(_drawn_inputs(seed))
    spreads = {'L0_attn_bq': (0.0, 0.8),
     'L0_attn_bk': (0.0, 0.8),
     'L0_attn_bv': (0.0, 0.461),
     'L0_attn_bo': (0.0, 0.1),
     'L0_ffn_in_proj_b': (0.0, 0.48),
     'L0_ffn_out_proj_b': (0.0, 0.1),
     'L0_ffn_ln1_g': (1.0, 0.2),
     'L0_ffn_ln1_b': (0.0, 0.1),
     'L0_ffn_ln2_g': (1.0, 0.2),
     'L0_ffn_ln2_b': (0.0, 0.1),
     'L0_ffn_b1': (0.0, 0.8),
     'L0_ffn_b2': (0.0, 0.8)}
    factors = {'L0_attn_Wq': 8.0,
     'L0_attn_Wk': 8.0,
     'L0_ffn_in_proj_w': 2.893,
     'L0_ffn_wg': 2.727,
     'L0_ffn_w1': 2.956,
     'L0_ffn_w2': 2.824}
    for name, (base, spread) in spreads.items():
        noise = np.random.default_rng([zlib.crc32(name.encode()), seed]).standard_normal(out[name].shape)
        drawn = base * np.exp(spread * noise) if base else spread * noise
        out[name] = jnp.asarray(drawn.astype(out[name].dtype))
    for name, factor in factors.items():
        out[name] = (out[name] * factor).astype(out[name].dtype)
    return out
```

```python
from contextlib import ExitStack

import concourse.bass as bass
from concourse import mybir

F32 = mybir.dt.float32
BF16 = mybir.dt.bfloat16
ALU = mybir.AluOpType
ACT = mybir.ActivationFunctionType
AX = mybir.AxisListType

P = 128
B, S, D = 8, 1024, 256
NB = P // B
T = S // NB
CH = D // P
H, C = 16, 64
HID = H * C
HH = H // 2
HC = HH * C
MH = 4
E, FF = 8, 1024
FC = FF // P
CAP = B * S // E
EPS = 1e-5
NEG = -1e30

SPLIT = 52
ROWS = C - SPLIT
GROUPS = [(0, 4), (44, 8)] + [g for j in range(4, 24, 4) for g in ((j, 4), (44 - j, 4))]
NG = len(GROUPS)
SLOTS, VSLOTS = 4, 4
RB = 4
NRB = ROWS // RB
assert NG % SLOTS == 0 and NG % VSLOTS == 0 and ROWS == NG and sum(nj for _, nj in GROUPS) == SPLIT
FT = 4


def size(g):
    j0, nj = GROUPS[g]
    return nj * HH * (SPLIT - j0)


def slot_size(i, slots):
    return max(size(g) for g in range(i, NG, slots))



def build(nc, x, Wq, bq, Wk, bk, Wv, bv, Wo, bo, in_w, in_b, out_w, out_b, g1, be1, g2, be2, wg, w1, b1, w2, b2, out):
    with ExitStack() as ctx:
        def sb(name, shape, dt=F32):
            return ctx.enter_context(nc.sbuf_tensor("sb_" + name, shape, dt))

        def ps(name):
            return ctx.enter_context(nc.psum_tensor("ps_" + name, [P, 512], F32))

        def sems(names):
            return [ctx.enter_context(nc.semaphore(n)) for n in names.split()]

        wqkv = sb("wqkv", [P, CH, 3, HID])
        wo = sb("wo", [P, HID // P, D])
        winT = sb("winT", [P, CH, 3 * D])
        woutT = sb("woutT", [P, CH, D])
        wgate = sb("wgate", [P, CH, E])
        we = sb("we", [P, CH, E * D])
        BO = 3 * HID
        BV, BOUT, BE = BO + D, BO + 2 * D, BO + 3 * D
        NBIAS = BE + E * D
        bias3 = sb("bias3", [3, NBIAS], BF16)
        bias_qk = sb("bias_qk", [P, 4])
        b1T = sb("b1T", [P, FC, E])
        b1c = sb("b1c", [P, FC, 3])
        ones3 = sb("ones3", [3, P], BF16)
        ident = sb("ident", [P, P])
        same_n = sb("same_n", [P, P])
        earlier = sb("earlier", [P, P], BF16)
        entry = sb("entry", [P, P], BF16)
        before = sb("before", [P, P], BF16)
        gains = sb("gains", [P, 4, D])
        scan_max = sb("scan_max", [P, HC])
        scan_min = sb("scan_min", [P, HC])
        first_of = sb("first_of", [P, E])
        NJ = max(nj for _, nj in GROUPS)
        causal = sb("causal", [P, NJ, NJ])
        minus_half = sb("minus_half", [P, FT])
        minus_later = sb("minus_later", [3, 2])

        x_in = sb("x_in", [P, D])
        xT = sb("xT", [P, CH, P])
        x_res = sb("x_res", [P, D])
        k8 = [sb(f"k8_{i}", [P, HC]) for i in range(2)]
        negm = [sb(f"negm_{i}", [P, HC]) for i in range(2)]
        qrow = [sb(f"qrow_{i}", [P, HH, ROWS]) for i in range(2)]
        kmax = sb("kmax", [P, HC])
        kmin = sb("kmin", [P, HC])
        ARENA = sum(slot_size(i, SLOTS) for i in range(SLOTS)) + sum(slot_size(i, VSLOTS) for i in range(VSLOTS))
        arena = sb("arena", [P, max(ARENA, 5 * 2048)])
        prow = sb("prow", [P, ROWS, HH, C])
        drow = [sb(f"drow_{i}", [P, HH, ROWS]) for i in range(2)]
        nrow = sb("nrow", [P, HH, ROWS])
        rden = sb("rden", [P, HH, C])
        attn = sb("attn", [P, HH, C])
        attnT = sb("attnT", [P, HID // P, P])
        r1 = sb("r1", [P, D])
        x2 = sb("x2", [P, D])
        x2T = sb("x2T", [P, CH, P])
        qkT = sb("qkT", [P, 4, P])
        v2 = sb("v2", [P, D])
        sc = sb("sc", [P, MH, P])
        nmx = sb("nmx", [P, MH])
        den2 = sb("den2", [P, MH])
        rden2 = sb("rden2", [P, MH])
        pT = sb("pT", [P, MH, P])
        o2 = sb("o2", [P, D])
        o2T = sb("o2T", [P, CH, P])
        y1 = sb("y1", [P, D])
        y1T = sb("y1T", [P, CH, P])
        shifted, expd, first, gate = [sb(n, [P, E]) for n in ("shifted", "expd", "first", "gate")]
        lmax, lsum, fmax, lrec = [sb(n, [P, 1]) for n in ("lmax", "lsum", "fmax", "lrec")]
        z = sb("z", [P, D])
        st = sb("st", [P, 6])
        mv = sb("mv", [P, 2])
        var = sb("var", [P, 1])
        rstd = sb("rstd", [P, 1])
        chosen = sb("chosen", [P, T, E], BF16)
        keep = sb("keep", [P, T])
        keep4 = [sb(f"keep4_{i}", [P, FT]) for i in range(2)]
        st4 = sb("st4", [P, FT, 6])
        mv4 = sb("mv4", [P, FT, 2])
        var4 = sb("var4", [P, FT])
        rstd4 = sb("rstd4", [P, FT])

        prob, pv, at = [], [], 0
        for i in range(SLOTS):
            prob.append(arena[:, at:at + slot_size(i, SLOTS)])
            at += slot_size(i, SLOTS)
        for i in range(VSLOTS):
            pv.append(arena[:, at:at + slot_size(i, VSLOTS)])
            at += slot_size(i, VSLOTS)
        wide = [arena[:, i * 2048:(i + 1) * 2048] for i in range(5)]
        w1s = [wide[i].rearrange("p (c f) -> p c f", c=CH) for i in range(2)]
        w2s = [wide[2 + i].rearrange("p (c d) -> p c d", c=FC) for i in range(2)]
        w1T = wide[4].rearrange("p (c d) -> p c d", c=FC)
        in_w_raw = wide[0][:, 0:6 * D].rearrange("p (r d) -> p r d", d=D)
        out_w_raw = wide[1][:, 0:2 * D].rearrange("p (r d) -> p r d", d=D)
        b1_raw = wide[2][0:E, 0:FF]
        bqk_raw = wide[3][0:4, 0:P]
        b2_raw = wide[4][0:3, :]
        bias_raw = prow[:].rearrange("p r h c -> p (r h c)")[0:3, 0:NBIAS]
        last = [wqkv[:, i, :, :].rearrange("p a n -> p (a n)").rearrange("p (f c d) -> p f c d", f=FT, c=3)
                for i in range(2)]

        q_ps = [ps("q0"), ps("q1")]
        v_ps = [ps("v0"), ps("v1")]
        acc_d, acc_n = ps("acc_d"), ps("acc_n")
        post, pre = ps("post"), ps("pre")

        scratch = nc.dram_tensor("scratch", [T, P, 3, D], F32, kind="Internal").ap()

        (consts_ready, loaded_w, loaded_bias, loaded_raw, loaded_gain, loaded_e0, loaded_e1, raw_ps, raw_sb,
         w1T_ps, w1T_sb, b1c_ready, we_ps, we_sb, bias_ready, rows_zero, pool_seq, dve_seq) = sems(
            "consts_ready loaded_w loaded_bias loaded_raw loaded_gain loaded_e0 loaded_e1 raw_ps raw_sb "
            "w1T_ps w1T_sb b1c_ready we_ps we_sb bias_ready rows_zero pool_seq dve_seq")
        (x_loaded, xT_ps, xT_sb, k_ps, k_sb, q_ready, v_ready, kscan, mprod, m_ready, qrow_ready,
         b_done, a_added, a_done, p_done, e_done, d_done, f_done, row_done, rowe_done, rowf_done,
         recip_done, finish_done) = sems(
            "x_loaded xT_ps xT_sb k_ps k_sb q_ready v_ready kscan mprod m_ready qrow_ready "
            "b_done a_added a_done p_done e_done d_done f_done row_done rowe_done rowf_done "
            "recip_done finish_done")
        (at_ps, at_sb, wo_ps, res_loaded, r_done, ln_stats, ln_mean, var_ready, rstd_ready, x2_done, x2_stored,
         x2T_ps, x2T_sb, qk_ps, qk_sb, v2_ps, v2_sb, sc_even, sc_ps, sc_masked, max_done, exp2_done, pT_ps, pT_sb,
         pv2_ps, rden2_done, o2_done, o2T_ps, o2T_sb, out_ps, y1_norm, y1_gain, y1_done, y1_stored, y1T_ps, y1T_sb,
         gate_ps, lmax_done, shifted_done, lsum_done, first_done, fmax_done, chosen_done, gate_done,
         moe_ps, z_added, z_stored) = sems(
            "at_ps at_sb wo_ps res_loaded r_done ln_stats ln_mean var_ready rstd_ready x2_done x2_stored "
            "x2T_ps x2T_sb qk_ps qk_sb v2_ps v2_sb sc_even sc_ps sc_masked max_done exp2_done pT_ps pT_sb "
            "pv2_ps rden2_done o2_done o2T_ps o2T_sb out_ps y1_norm y1_gain y1_done y1_stored y1T_ps y1T_sb "
            "gate_ps lmax_done shifted_done lsum_done first_done fmax_done chosen_done gate_done "
            "moe_ps z_added z_stored")
        (rank_ps, rank_seq, keep_done, tiles_loaded0, tiles_loaded1, fin_seq, fin_var, fin_rstd, fin_out,
         out_stored0, out_stored1) = sems(
            "rank_ps rank_seq keep_done tiles_loaded0 tiles_loaded1 fin_seq fin_var fin_rstd fin_out "
            "out_stored0 out_stored1")
        loaded_e = [loaded_e0, loaded_e1]
        tiles_loaded = [tiles_loaded0, tiles_loaded1]
        out_stored = [out_stored0, out_stored1]

        xt = x.rearrange("l (t n) d -> t l n d", n=NB)
        outt = out.rearrange("l (t n) d -> t l n d", n=NB)

        def tile_of(ap, i):
            if isinstance(i, int):
                return ap[i]
            sub = ap[bass.ds(i, 1)]
            return sub.rearrange("a p c d -> (a p) c d")

        def by_head(ap, w=C):
            return ap.rearrange("p (h c) -> p h c", c=w)

        def group(buf, g):
            j0, nj = GROUPS[g]
            return buf[:, 0:size(g)].rearrange("p (j h i) -> p j h i", j=nj, h=HH)

        def row(ap):
            return ap.rearrange("(a n) -> a n", a=1)

        PLAN = {
            "pe": [{4: ["at"], 5: ["wo"], 6: ["pre_k"], 7: ["x2", "pre_q"], 8: ["qk"], 9: ["v2", "pre_v"], 10: ["sc"]},
                   {0: ["pT"], 1: ["pv2"], 2: ["o2T", "pre_x"], 3: ["out"], 4: ["at"], 5: ["y1T", "pre_k"],
                    6: ["gate", "pre_q"], 7: ["moe0"], 8: ["pre_v"], 9: ["moe1"]}],
            "act": [{4: ["at"], 6: ["pre_k"], 7: ["x2"], 9: ["v2"], 11: ["exp2"]},
                    {0: ["pT"], 2: ["o2T", "pre_x"], 4: ["at"], 5: ["y1T", "pre_k"], 6: ["gate"]}],
            "dve": [{3: ["fin"], 5: ["r"], 6: ["x2"], 7: ["pre_k"], 8: ["pre_q", "qk"], 9: ["pre_m"], 10: ["sc"]},
                    {0: ["pT"], 1: ["pv2"], 3: ["fin", "r2"], 4: ["y1"], 6: ["gate", "pre_k"], 7: ["pre_q", "gate_"],
                     8: ["pre_m", "moe0"], 10: ["moe1"]}],
            "pool": [{5: ["r"]}, {3: ["r2"]}],
        }

        def stages(eng, half, k, old, post_tile, next_half):
            for name in PLAN[eng][half].get(k, []):
                if next_half if name.startswith("pre") else old if name in ("fin", "at") else post_tile:
                    yield name

        def all_periods(eng, period):
            period(0, 0, new=True, old=False, post_tile=False, next_half=True)
            period(0, 1, new=True, old=True, post_tile=False, next_half=True)
            with eng.Fori(1, T - 1) as t:
                period(t, 0, new=True, old=True, post_tile=True, next_half=True)
                period(t, 1, new=True, old=True, post_tile=True, next_half=True)
            period(T - 1, 0, new=True, old=True, post_tile=True, next_half=True)
            period(T - 1, 1, new=True, old=True, post_tile=True, next_half=False)
            period(T, 0, new=False, old=True, post_tile=True, next_half=False)
            period(T, 1, new=False, old=False, post_tile=True, next_half=False)

        def behind(t, half, k, lag):
            if k >= lag:
                return t, half, k - lag
            return (t, 0, k - lag + NG) if half else (t - 1, 1, k - lag + NG)

        def halves(t, half):
            return t * 2 + half

        def nth(t, half, g):
            return t * (2 * NG) + (half * NG + g + 1)

        def wait(eng, sem, value):
            if not isinstance(value, int) or value > 0:
                eng.wait_ge(sem, value)

        block = ctx.enter_context(nc.Block())

        @block.sync
        def _(sp):
            for i, w in enumerate((Wq, Wk, Wv)):
                sp.dma_start(wqkv[:, :, i, :], w.rearrange("(c p) n -> p c n", p=P)).then_inc(loaded_w, 16)
            sp.dma_start(x_in[:], xt[0]).then_inc(x_loaded, 16)
            sp.dma_start(in_w_raw, in_w.rearrange("(r p) d -> p r d", p=P)).then_inc(loaded_raw, 16)
            sp.dma_start(out_w_raw, out_w.rearrange("(r p) d -> p r d", p=P)).then_inc(loaded_raw, 16)
            sp.dma_start(b1_raw, b1).then_inc(loaded_raw, 16)
            sp.dma_start(bqk_raw, in_b[0:2 * D].rearrange("(r p) -> r p", p=P)).then_inc(loaded_raw, 16)
            for part in range(3):
                for src, at in ((bq, 0), (bk, HID), (bv, 2 * HID), (bo, BO), (in_b[2 * D:3 * D], BV), (out_b, BOUT)):
                    sp.dma_start(bias_raw[part:part + 1, at:at + src.shape[0]], row(src)).then_inc(loaded_bias, 16)
                sp.dma_start(b2_raw[part:part + 1, :], row(b2.rearrange("e d -> (e d)"))).then_inc(loaded_bias, 16)
            sp.dma_start(wo[:], Wo.rearrange("(c p) n -> p c n", p=P)).then_inc(loaded_w, 16)
            sp.dma_start(wgate[:], wg.rearrange("(c p) e -> p c e", p=P)).then_inc(loaded_w, 16)
            for i, src in enumerate((g1, be1, g2, be2)):
                sp.dma_start(gains[:, i, :], row(src).broadcast_to([P, D])).then_inc(loaded_gain, 16)
            sp.wait_ge(raw_sb, 6)
            for e in range(2):
                sp.dma_start(w1s[e], w1[e].rearrange("(c p) f -> p c f", p=P)).then_inc(loaded_e[e], 16)
                sp.dma_start(w2s[e], w2[e].rearrange("(c p) d -> p c d", p=P)).then_inc(loaded_e[e], 16)
            with sp.Fori(1, E // 2) as pair:
                for i in range(2):
                    e = pair * 2 + i
                    sp.wait_ge(we_ps, pair * 2 + (i - 1))
                    sp.dma_start(w1s[i], tile_of(w1.rearrange("e (c p) f -> e p c f", p=P), e)).then_inc(loaded_e[i], 16)
                    sp.dma_start(w2s[i], tile_of(w2.rearrange("e (c p) d -> e p c d", p=P), e)).then_inc(loaded_e[i], 16)

            def period(t, half, new, old, post_tile, next_half):
                if half == 0 and new and next_half and not (isinstance(t, int) and t == T - 1):
                    sp.wait_ge(xT_ps, t + 1)
                    sp.dma_start(x_in[:], tile_of(xt, t + 1)).then_inc(x_loaded, 16)
                if not post_tile:
                    return
                if half == 0:
                    wait(sp, r_done, t * 2 - 2)
                    sp.dma_start(x_res[:], tile_of(xt, t - 1)).then_inc(res_loaded, 16)
                    sp.wait_ge(x2_done, t)
                    sp.dma_start(tile_of(scratch, t - 1)[:, 0, :], x2[:]).then_inc(x2_stored, 16)
                else:
                    sp.wait_ge(y1_done, t)
                    sp.dma_start(tile_of(scratch, t - 1)[:, 1, :], y1[:]).then_inc(y1_stored, 16)
                    sp.wait_ge(z_added, t * 8)
                    sp.dma_start(tile_of(scratch, t - 1)[:, 2, :], z[:]).then_inc(z_stored, 16)

            all_periods(sp, period)

            sp.wait_ge(x2_stored, 16 * T)
            sp.wait_ge(y1_stored, 16 * T)
            sp.wait_ge(z_stored, 16 * T)
            sp.wait_ge(rank_ps, 3)

            def load(i, b):
                sp.dma_start(last[i].rearrange("p f c d -> p f (c d)"),
                             scratch[bass.ds(b * FT, FT)].rearrange("t p c d -> p t (c d)")).then_inc(tiles_loaded[i], 16)

            def store(i, b):
                sp.wait_ge(fin_out, b + 1)
                for f in range(FT):
                    sp.dma_start(tile_of(outt, b * FT + f), last[i][:, f, 0, :]).then_inc(out_stored[i], 16)

            load(0, 0)
            load(1, 1)
            with sp.Fori(0, T // FT // 2 - 1) as pair:
                for i in range(2):
                    store(i, pair * 2 + i)
                    sp.wait_ge(out_stored[i], pair * (16 * FT) + 16 * FT)
                    load(i, pair * 2 + (i + 2))
            for i in range(2):
                store(i, T // FT - 2 + i)
            for i in range(2):
                sp.wait_ge(out_stored[i], 16 * FT * (T // FT // 2))

        @block.gpsimd
        def _(pool):
            done = [0]

            def link(ins):
                ins.then_inc(pool_seq, 1)
                done[0] += 1
                pool.wait_ge(pool_seq, done[0])

            link(nc.gpsimd.memset(ident[:], 1.0))
            link(nc.gpsimd.affine_select(out=ident[:], in_=ident[:], compare_op=ALU.is_equal, fill=0.0, base=0,
                                         pattern=[[-1, P]], channel_multiplier=1))
            link(nc.gpsimd.memset(same_n[:], NEG))
            for l in range(-(B - 1), B):
                link(nc.gpsimd.affine_select(out=same_n[:], in_=same_n[:], compare_op=ALU.not_equal, fill=0.0,
                                             base=l * NB, pattern=[[-1, P]], channel_multiplier=1))
            blocks = [m[:].rearrange("p (l n) -> p l n", n=NB) for m in (entry, before)]
            link(nc.gpsimd.memset(entry[:], 1.0))
            link(nc.gpsimd.affine_select(out=blocks[0], in_=blocks[0], compare_op=ALU.is_ge, fill=0.0, base=0,
                                         pattern=[[-NB, B], [0, NB]], channel_multiplier=1))
            link(nc.gpsimd.affine_select(out=blocks[0], in_=blocks[0], compare_op=ALU.is_ge, fill=0.0, base=NB - 1,
                                         pattern=[[NB, B], [0, NB]], channel_multiplier=-1))
            link(nc.gpsimd.affine_select(out=earlier[:], in_=entry[:], compare_op=ALU.is_ge, fill=0.0, base=-1,
                                         pattern=[[1, P]], channel_multiplier=-1))
            link(nc.gpsimd.memset(before[:], 1.0))
            link(nc.gpsimd.affine_select(out=blocks[1], in_=blocks[1], compare_op=ALU.is_ge, fill=0.0, base=-1,
                                         pattern=[[NB, B], [0, NB]], channel_multiplier=-1))
            link(nc.gpsimd.memset(minus_later[:], -1.0))
            for part in range(2):
                link(nc.gpsimd.affine_select(out=minus_later[:, part:part + 1], in_=minus_later[:, part:part + 1],
                                             compare_op=ALU.is_ge, fill=0.0, base=-1 - part, pattern=[[0, 1]],
                                             channel_multiplier=1))
            link(nc.gpsimd.memset(minus_half[:], -0.5))
            link(nc.gpsimd.memset(causal[:], 0.0))
            link(nc.gpsimd.affine_select(out=causal[:], in_=causal[:], compare_op=ALU.is_ge, fill=NEG, base=0,
                                         pattern=[[-1, NJ], [1, NJ]], channel_multiplier=0))
            nc.gpsimd.memset(ones3[:], 1.0).then_inc(consts_ready, 1)
            pool.wait_ge(bias_ready, 2)
            nc.gpsimd.memset(prow[:], 0.0).then_inc(rows_zero, 1)

            def period(t, half, new, old, post_tile, next_half):
                for k in range(NG):
                    if new:
                        n, (j0, nj) = nth(t, half, k), GROUPS[k]
                        p = group(prob[k % SLOTS], k)
                        if k == 0:
                            pool.wait_ge(m_ready, halves(t, half) + 1)
                        pool.wait_ge(b_done, n)
                        nc.gpsimd.tensor_tensor(
                            p, p, by_head(negm[half][:])[:, :, j0:SPLIT].unsqueeze(1).broadcast_to([P, nj, HH, SPLIT - j0]),
                            ALU.add).then_inc(a_added, 1)
                        pool.wait_ge(a_added, n)
                        corner = p[:, :, :, 0:nj]
                        nc.gpsimd.tensor_tensor(corner, corner, causal[:, 0:nj, 0:nj].unsqueeze(2).broadcast_to([P, nj, HH, nj]),
                                                ALU.add).then_inc(a_done, 1)
                    for name in stages("pool", half, k, old, post_tile, next_half):
                        if name in ("r", "r2"):
                            pool.wait_ge(var_ready, t * 2 - (1 if name == "r" else 0))
                            nc.gpsimd.tensor_tensor(rstd[:], var[:], minus_half[:, 0:1], ALU.pow).then_inc(rstd_ready, 1)

            all_periods(pool, period)

            with pool.Fori(0, T // FT) as b:
                for i in range(2):
                    pool.wait_ge(fin_var, b * 2 + (i + 1))
                    nc.gpsimd.tensor_tensor(rstd4[:], var4[:], minus_half[:], ALU.pow).then_inc(fin_rstd, 1)

        @block.tensor
        def _(pe):
            mm = nc.tensor.matmul
            banks = q_ps + v_ps + [acc_d, acc_n]
            pe.wait_ge(consts_ready, 1)
            pe.wait_ge(loaded_raw, 64)
            for i in range(4):
                src, r0 = (in_w_raw, 2 * i) if i < 3 else (out_w_raw, 0)
                for r in range(2):
                    for c in range(CH):
                        a = (2 * r + c) * P
                        ins = nc.tensor.transpose(banks[i][:, a:a + P], src[:, r0 + r, c * P:(c + 1) * P], ident[:])
                ins.then_inc(raw_ps, 1)
            for c in range(FC):
                ins = nc.tensor.transpose(banks[4][:, c * E:(c + 1) * E], b1_raw[:, c * P:(c + 1) * P], ident[0:E, 0:E])
            ins.then_inc(raw_ps, 1)
            nc.tensor.transpose(banks[5][:, 0:4], bqk_raw, ident[0:4, 0:4]).then_inc(raw_ps, 1)
            pe.wait_ge(raw_sb, 6)
            with pe.Fori(0, E // 2) as pair:
                e0 = pair * 2
                for i in range(2):
                    pe.wait_ge(loaded_e[i], pair * 32 + 32)
                    for b in range(4):
                        for f in range(2):
                            for c in range(CH):
                                a = (2 * f + c) * P
                                ins = nc.tensor.transpose(banks[b][:, a:a + P],
                                                          w1s[i][:, c, (2 * b + f) * P:(2 * b + f + 1) * P], ident[:])
                        ins.then_inc(w1T_ps, 1)
                    pe.wait_ge(w1T_sb, e0 * 4 + (4 * i + 4))
                    pe.wait_ge(b1c_ready, e0 + (i + 1))
                    for c in range(CH):
                        for f in range(FC):
                            mm([acc_d, acc_n][c][:, 0:D], w1T[:, f, c * P:(c + 1) * P], w2s[i][:, f, :],
                               start=(f == 0), stop=(f == FC - 1))
                    for f in range(FC):
                        ins = mm(post[0:3, 0:D], b1c[:, f, :], w2s[i][:, f, :], start=(f == 0), stop=(f == FC - 1))
                    ins.then_inc(we_ps, 1)
                    pe.wait_ge(we_sb, e0 + (i + 1))

            def bias(bank, at, n):
                mm(bank[:, 0:n], ones3[:], bias3[:, at:at + n], start=True, stop=False)

            def project(bank, half, which):
                bias(bank, which * HID + half * HC, HC)
                for c in range(CH):
                    ins = mm(bank[:], xT[:, c, :], wqkv[:, c, which, half * HC:(half + 1) * HC], start=False, stop=(c == CH - 1))
                return ins

            def prepare(name, t, half):
                tn, hn = (t, 1) if half == 0 else (t + 1, 0)
                n = halves(tn, hn)
                if name == "pre_x":
                    pe.wait_ge(x_loaded, tn * 16 + 16)
                    wait(pe, k_sb, n)
                    for c in range(CH):
                        ins = nc.tensor.transpose(pre[:, c * P:(c + 1) * P], x_in[:, c * P:(c + 1) * P], ident[:])
                    ins.then_inc(xT_ps, 1)
                if name == "pre_k":
                    if hn == 0:
                        pe.wait_ge(xT_sb, tn + 1)
                    else:
                        wait(pe, z_added, t * 8 - 8)
                        wait(pe, k_sb, n)
                    project(pre, hn, 1).then_inc(k_ps, 1)
                if name == "pre_q":
                    wait(pe, qrow_ready, n - 1)
                    wait(pe, b_done, nth(t, half, 0) - 1)
                    wait(pe, m_ready, n - 1)
                    project(q_ps[hn], hn, 0).then_inc(q_ready, 1)
                if name == "pre_v":
                    wait(pe, e_done, nth(t, half, 0) - 1)
                    wait(pe, rowe_done, n * NRB - NRB)
                    project(v_ps[hn], hn, 2).then_inc(v_ready, 1)

            def sums(t, half, g, acc, buf, ready, done):
                pe.wait_ge(ready, nth(t, half, g))
                nj, j0 = GROUPS[g][1], GROUPS[g][0]
                for j in range(nj):
                    ins = mm(by_head(acc[:])[:, :, j0:SPLIT], ident[:], group(buf, g)[:, j], start=(g == 0 and j == 0),
                             stop=(g == NG - 1 and j == nj - 1), skip_group_check=True)
                ins.then_inc(done, 1)

            def denominators(t, half, g):
                if g == 0:
                    wait(pe, recip_done, halves(t, half))
                sums(t, half, g, acc_d, prob[g % SLOTS], p_done, d_done)

            def numerators(t, half, g):
                if g == 0:
                    wait(pe, finish_done, halves(t, half))
                sums(t, half, g, acc_n, pv[g % VSLOTS], e_done, f_done)

            def transposes(bank, src, n, done):
                for c in range(n):
                    ins = nc.tensor.transpose(bank[:, c * P:(c + 1) * P], src(c), ident[:])
                ins.then_inc(done, 1)

            def work(name, t, half):
                if name == "at":
                    pe.wait_ge(finish_done, halves(t, half))
                    if half == 0:
                        wait(pe, z_added, t * 8 - 8)
                    else:
                        wait(pe, r_done, t * 2)
                    transposes(post, lambda c: attn[:].rearrange("p h c -> p (h c)")[:, c * P:(c + 1) * P], 4, at_ps)
                if name == "wo":
                    pe.wait_ge(at_sb, t * 2)
                    bias(post, BO, D)
                    for c in range(HID // P):
                        ins = mm(post[:, 0:D], attnT[:, c, :], wo[:, c, :], start=False, stop=(c == HID // P - 1))
                    ins.then_inc(wo_ps, 1)
                if name == "x2":
                    pe.wait_ge(x2_done, t)
                    transposes(post, lambda c: x2[:, c * P:(c + 1) * P], CH, x2T_ps)
                if name == "qk":
                    pe.wait_ge(x2T_sb, t)
                    for m in range(4):
                        for c in range(CH):
                            ins = mm(post[:, m * P:(m + 1) * P], winT[:, c, m * P:(m + 1) * P], x2T[:, c, :],
                                     start=(c == 0), stop=(c == CH - 1))
                    ins.then_inc(qk_ps, 1)
                if name == "v2":
                    pe.wait_ge(qk_sb, t)
                    bias(post, BV, D)
                    for c in range(CH):
                        ins = mm(post[:, 0:D], x2T[:, c, :], winT[:, c, 2 * D:3 * D], start=False, stop=(c == CH - 1))
                    ins.then_inc(v2_ps, 1)
                if name == "sc":
                    pe.wait_ge(v2_sb, t)
                    for a in (0, 64):
                        if a:
                            pe.wait_ge(sc_even, t)
                        for m in range(2):
                            h = 2 * m + a // 64
                            ins = mm(post[:, h * P:(h + 1) * P], qkT[a:a + 64, m, :], qkT[a:a + 64, 2 + m, :],
                                     start=True, stop=True)
                        ins.then_inc(sc_ps if a else sc_even, 1)
                if name == "pT":
                    pe.wait_ge(exp2_done, t)
                    transposes(post, lambda h: sc[:, h, :], MH, pT_ps)
                if name == "pv2":
                    pe.wait_ge(pT_sb, t)
                    for h in range(MH):
                        ins = mm(post[:, h * 64:(h + 1) * 64], pT[:, h, :], v2[:, h * 64:(h + 1) * 64], start=True, stop=True)
                    ins.then_inc(pv2_ps, 1)
                if name == "o2T":
                    pe.wait_ge(o2_done, t)
                    transposes(post, lambda c: o2[:, c * P:(c + 1) * P], CH, o2T_ps)
                if name == "out":
                    pe.wait_ge(o2T_sb, t)
                    bias(post, BOUT, D)
                    for c in range(CH):
                        ins = mm(post[:, 0:D], o2T[:, c, :], woutT[:, c, :], start=False, stop=(c == CH - 1))
                    ins.then_inc(out_ps, 1)
                if name == "y1T":
                    pe.wait_ge(y1_done, t)
                    pe.wait_ge(at_sb, 2 * T if isinstance(t, int) and t == T else t * 2 + 1)
                    transposes(post, lambda c: y1[:, c * P:(c + 1) * P], CH, y1T_ps)
                if name == "gate":
                    pe.wait_ge(y1T_sb, t)
                    for c in range(CH):
                        ins = mm(post[:, 0:E], y1T[:, c, :], wgate[:, c, :], start=(c == 0), stop=(c == CH - 1))
                    ins.then_inc(gate_ps, 1)
                if name in ("moe0", "moe1"):
                    m = int(name[3])
                    for i, bank in enumerate((post, pre)):
                        c4 = 2 * m + i
                        if m == 1:
                            pe.wait_ge(z_added, t * 8 - 8 + 2 * (i + 1))
                        elif i == 0:
                            pe.wait_ge(shifted_done, t)
                        else:
                            pe.wait_ge(k_sb, 2 * T if isinstance(t, int) and t >= T - 1 else halves(t, half) + 2)
                        bias(bank, BE + c4 * 512, 512)
                        for c in range(CH):
                            ins = mm(bank[:], y1T[:, c, :], we[:, c, c4 * 512:(c4 + 1) * 512], start=False, stop=(c == CH - 1))
                        ins.then_inc(moe_ps, 1)

            pe.wait_ge(loaded_w, 80)
            pe.wait_ge(bias_ready, 2)
            prepare("pre_x", -1, 1)
            for name in ("pre_k", "pre_q", "pre_v"):
                prepare(name, -1, 1)

            def period(t, half, new, old, post_tile, next_half):
                for k in range(NG):
                    if new if k >= 3 else old:
                        denominators(*behind(t, half, k, 3))
                    for name in stages("pe", half, k, old, post_tile, next_half):
                        prepare(name, t, half)
                        work(name, t, half)
                    if new if k >= 4 else old:
                        numerators(*behind(t, half, k, 4))

            all_periods(pe, period)

            pe.wait_ge(chosen_done, T)
            pe.wait_ge(m_ready, 2 * T)
            pe.wait_ge(e_done, 2 * T * NG)
            for m, bank in zip((earlier, entry, before), (q_ps[0], q_ps[1], v_ps[0])):
                mm(bank[:], m[:], chosen[:].rearrange("p t e -> p (t e)"), start=True, stop=True).then_inc(rank_ps, 1)

        @block.scalar
        def _(act):
            go = nc.scalar.activation
            banks = q_ps + v_ps + [acc_d, acc_n]
            for i in range(4):
                act.wait_ge(raw_ps, i + 1)
                dst = winT[:, :, 2 * i * P:(2 * i + 2) * P] if i < 3 else woutT[:]
                nc.scalar.copy(dst.rearrange("p c (r n) -> p r c n", n=P),
                               banks[i][:].rearrange("p (r c n) -> p r c n", r=2, c=CH)).then_inc(raw_sb, 1)
            act.wait_ge(raw_ps, 5)
            nc.scalar.copy(b1T[:], banks[4][:, 0:FC * E].rearrange("p (c e) -> p c e", e=E)).then_inc(raw_sb, 1)
            act.wait_ge(raw_ps, 6)
            nc.scalar.copy(bias_qk[:], banks[5][:, 0:4]).then_inc(raw_sb, 1)
            act.wait_ge(raw_sb, 6)
            act.wait_ge(bias_ready, 1)
            with act.Fori(0, E // 2) as pair:
                e0 = pair * 2
                for i in range(2):
                    for b in range(4):
                        act.wait_ge(w1T_ps, e0 * 4 + (4 * i + b + 1))
                        nc.scalar.copy(w1T[:, 2 * b:2 * b + 2, :].rearrange("p f (c n) -> p f c n", n=P),
                                       banks[b][:].rearrange("p (f c n) -> p f c n", f=2, c=CH)).then_inc(w1T_sb, 1)
                    nc.scalar.copy(b1c[:], b1T[:, :, bass.ds(e0 + i, 1)].broadcast_to([P, FC, 3])).then_inc(b1c_ready, 1)
                    act.wait_ge(we_ps, e0 + (i + 1))
                    for c in range(CH):
                        nc.scalar.copy(we[:, c, bass.ds((e0 + i) * D, D)], [acc_d, acc_n][c][:, 0:D])
                    nc.scalar.copy(bias_raw[:, bass.ds((e0 + i) * D + BE, D)], post[0:3, 0:D]).then_inc(we_sb, 1)

            def copy_out(ps_sem, n, dst, src, done):
                act.wait_ge(ps_sem, n)
                nc.scalar.copy(dst, src).then_inc(done, 1)

            def prepare(name, t, half):
                tn, hn = (t, 1) if half == 0 else (t + 1, 0)
                n = halves(tn, hn)
                if name == "pre_x":
                    copy_out(xT_ps, tn + 1, xT[:].rearrange("p c n -> p (c n)"), pre[:, 0:D], xT_sb)
                if name == "pre_k":
                    act.wait_ge(k_ps, n + 1)
                    wait(act, b_done, nth(t, half, 0) - 1)
                    wait(act, kscan, n * 2 - 2)
                    nc.scalar.mul(k8[hn][:], pre[:], 0.125).then_inc(k_sb, 1)

            def work(name, t):
                if name == "exp2":
                    act.wait_ge(max_done, t)
                    for h in range(MH):
                        ins = go(sc[:, h, :], sc[:, h, :], ACT.Exp, bias=nmx[:, h:h + 1], accum_out=den2[:, h:h + 1])
                    ins.then_inc(exp2_done, 1)
                if name == "x2":
                    copy_out(x2T_ps, t, x2T[:].rearrange("p c n -> p (c n)"), post[:, 0:D], x2T_sb)
                if name == "v2":
                    copy_out(v2_ps, t, v2[:], post[:, 0:D], v2_sb)
                if name == "pT":
                    copy_out(pT_ps, t, pT[:].rearrange("p h n -> p (h n)"), post[:], pT_sb)
                if name == "o2T":
                    copy_out(o2T_ps, t, o2T[:].rearrange("p c n -> p (c n)"), post[:, 0:D], o2T_sb)
                if name == "y1T":
                    copy_out(y1T_ps, t, y1T[:].rearrange("p c n -> p (c n)"), post[:, 0:D], y1T_sb)
                if name == "gate":
                    act.wait_ge(shifted_done, t)
                    go(expd[:], shifted[:], ACT.Exp, accum_out=lsum[:]).then_inc(lsum_done, 1)

            prepare("pre_x", -1, 1)
            prepare("pre_k", -1, 1)
            act.wait_ge(rows_zero, 1)

            def period(t, half, new, old, post_tile, next_half):
                for k in range(NG):
                    if new if k >= 1 else old:
                        te, he, g = behind(t, half, k, 1)
                        act.wait_ge(a_done, nth(te, he, g))
                        p = prob[g % SLOTS]
                        go(p, p, ACT.Exp).then_inc(p_done, 1) if size(g) == p.shape[1] else \
                            go(p[:, 0:size(g)], p[:, 0:size(g)], ACT.Exp).then_inc(p_done, 1)
                    if new:
                        n, i = halves(t, half), SPLIT + k
                        if k == 0:
                            act.wait_ge(k_sb, n + 1)
                            act.wait_ge(qrow_ready, n + 1)
                            act.wait_ge(m_ready, n + 1)
                            wait(act, finish_done, n - 1)
                        if k % RB == 0:
                            wait(act, rowf_done, n * NRB - NRB + (k // RB + 1))
                        for h in range(HH):
                            ins = go(prow[:, k, h, 0:i + 1], k8[half][:, h * C:h * C + i + 1], ACT.Exp,
                                     bias=negm[half][:, h * C + i:h * C + i + 1], scale=qrow[half][:, h, k:k + 1],
                                     accum_out=drow[half][:, h, k:k + 1])
                        ins.then_inc(row_done, 1)
                    for name in stages("act", half, k, old, post_tile, next_half):
                        if name == "at":
                            c0 = 4 * (1 - half)
                            if half == 1:
                                wait(act, wo_ps, t)
                            copy_out(at_ps, halves(t, half), attnT[:, c0:c0 + 4, :].rearrange("p c n -> p (c n)"), post[:], at_sb)
                        prepare(name, t, half)
                        work(name, t)

            all_periods(act, period)

        @block.vector
        def _(dve):
            tt, stt, ts = nc.vector.tensor_tensor, nc.vector.scalar_tensor_tensor, nc.vector.tensor_scalar
            done = [0]

            def link(ins):
                ins.then_inc(dve_seq, 1)
                done[0] += 1
                dve.wait_ge(dve_seq, done[0])

            link(nc.vector.memset(scan_max[:], 0.0))
            link(nc.vector.memset(scan_min[:], 0.0))
            nc.vector.memset(by_head(scan_max[:])[:, :, 0:1], NEG)
            nc.vector.memset(by_head(scan_min[:])[:, :, 0:1], -NEG)
            for e in range(E):
                ins = nc.vector.memset(first_of[:, e:e + 1], float(E - e))
            link(ins)

            def split(a, b):
                link(nc.vector.tensor_copy(bias3[:, a:b], bias_raw[:, a:b]))
                for part in range(2):
                    link(stt(out=bias_raw[:, a:b], in0=bias3[:, a:b], scalar=minus_later[:, part:part + 1], in1=bias_raw[:, a:b],
                             op0=ALU.mult, op1=ALU.add))
                    ins = nc.vector.tensor_copy(bias3[:, a:b], bias_raw[:, a:b])
                    if part == 0:
                        link(ins)
                return ins

            dve.wait_ge(consts_ready, 1)
            dve.wait_ge(loaded_bias, 3 * 7 * 16)
            keep_b2 = [k8[0], k8[1], kmax, kmin]
            for i, buf in enumerate(keep_b2):
                nc.vector.tensor_copy(buf[0:3, :], b2_raw[:, i * 512:(i + 1) * 512])
            split(0, BE).then_inc(bias_ready, 1)
            dve.wait_ge(bias_ready, 1)
            dve.wait_ge(we_sb, E)
            for i, buf in enumerate(keep_b2):
                part = bias_raw[:, BE + i * 512:BE + (i + 1) * 512]
                ins = tt(part, part, buf[0:3, :], ALU.add)
            link(ins)
            split(BE, NBIAS).then_inc(bias_ready, 1)
            dve.wait_ge(loaded_gain, 64)

            def prepare(name, t, half):
                tn, hn = (t, 1) if half == 0 else (t + 1, 0)
                n = halves(tn, hn)
                if name == "pre_k":
                    dve.wait_ge(k_sb, n + 1)
                    nc.vector.tensor_tensor_scan(kmax[:], scan_max[:], k8[hn][:], 0.0, ALU.add, ALU.max).then_inc(kscan, 1)
                    nc.vector.tensor_tensor_scan(kmin[:], scan_min[:], k8[hn][:], 0.0, ALU.add, ALU.min).then_inc(kscan, 1)
                if name == "pre_q":
                    dve.wait_ge(q_ready, n + 1)
                    wait(dve, row_done, n * ROWS - ROWS)
                    nc.vector.tensor_copy(qrow[hn][:], by_head(q_ps[hn][:])[:, :, SPLIT:C]).then_inc(qrow_ready, 1)
                    dve.wait_ge(kscan, n * 2 + 2)
                    for buf in (kmax, kmin):
                        stt(out=buf[:], in0=q_ps[hn][:], scalar=-1.0, in1=buf[:], op0=ALU.mult, op1=ALU.mult).then_inc(mprod, 1)
                if name == "pre_m":
                    dve.wait_ge(mprod, n * 2 + 2)
                    wait(dve, a_added, nth(t, half, 0) - 1)
                    tt(negm[hn][:], kmax[:], kmin[:], ALU.min).then_inc(m_ready, 1)

            def product(t, half, g):
                (j0, nj), n = GROUPS[g], nth(t, half, g)
                w = SPLIT - j0
                if g == 0:
                    dve.wait_ge(q_ready, halves(t, half) + 1)
                    dve.wait_ge(k_sb, halves(t, half) + 1)
                wait(dve, d_done, n - SLOTS)
                wait(dve, e_done, n - SLOTS)
                tt(group(prob[g % SLOTS], g),
                   by_head(q_ps[half][:])[:, :, j0:SPLIT].unsqueeze(1).broadcast_to([P, nj, HH, w]),
                   by_head(k8[half][:])[:, :, j0:j0 + nj].rearrange("p h j -> p j h").unsqueeze(3).broadcast_to([P, nj, HH, w]),
                   ALU.mult).then_inc(b_done, 1)

            def times_v(t, half, g):
                (j0, nj), n = GROUPS[g], nth(t, half, g)
                w = SPLIT - j0
                if g == 0:
                    dve.wait_ge(v_ready, halves(t, half) + 1)
                dve.wait_ge(p_done, n)
                wait(dve, f_done, n - VSLOTS)
                tt(group(pv[g % VSLOTS], g), group(prob[g % SLOTS], g),
                   by_head(v_ps[half][:])[:, :, j0:j0 + nj].rearrange("p h j -> p j h").unsqueeze(3).broadcast_to([P, nj, HH, w]),
                   ALU.mult).then_inc(e_done, 1)

            def rows_times_v(t, half, b):
                dve.wait_ge(v_ready, halves(t, half) + 1)
                dve.wait_ge(row_done, halves(t, half) * ROWS + (b + 1) * RB)
                p = prow[:, b * RB:(b + 1) * RB]
                tt(p, p, by_head(v_ps[half][:]).unsqueeze(1).broadcast_to([P, RB, HH, C]), ALU.mult).then_inc(rowe_done, 1)

            def rows_sum(t, half, b):
                dve.wait_ge(rowe_done, halves(t, half) * NRB + (b + 1))
                nc.vector.tensor_reduce(nrow[:, :, b * RB:(b + 1) * RB].rearrange("p h r -> p r h"),
                                        prow[:, b * RB:(b + 1) * RB], AX.X, ALU.add).then_inc(rowf_done, 1)

            def reciprocals(t, half):
                n = halves(t, half)
                other = 1 - half
                dve.wait_ge(d_done, n * NG)
                dve.wait_ge(row_done, n * ROWS)
                nc.vector.reciprocal(rden[:, :, 0:SPLIT], by_head(acc_d[:])[:, :, 0:SPLIT])
                nc.vector.reciprocal(rden[:, :, SPLIT:C], drow[other][:]).then_inc(recip_done, 1)

            def finish(t, half):
                n = halves(t, half)
                dve.wait_ge(recip_done, n)
                dve.wait_ge(f_done, n * NG)
                dve.wait_ge(rowf_done, n * NRB)
                wait(dve, at_ps, n - 1)
                tt(attn[:, :, 0:SPLIT], by_head(acc_n[:])[:, :, 0:SPLIT], rden[:, :, 0:SPLIT], ALU.mult)
                tt(attn[:, :, SPLIT:C], nrow[:], rden[:, :, SPLIT:C], ALU.mult).then_inc(finish_done, 1)

            def layer_stats(n):
                dve.wait_ge(r_done, n)
                nc.vector.bn_stats(st[:], r1[:]).then_inc(ln_stats, 1)
                dve.wait_ge(ln_stats, n)
                nc.vector.memset(var[:], EPS)
                nc.vector.bn_aggr(mv[:], st[:]).then_inc(ln_mean, 1)
                dve.wait_ge(ln_mean, n)
                tt(var[:], mv[:, 1:2], var[:], ALU.add).then_inc(var_ready, 1)

            def work(name, t):
                if name == "r":
                    dve.wait_ge(wo_ps, t)
                    dve.wait_ge(res_loaded, t * 16)
                    tt(r1[:], post[:, 0:D], x_res[:], ALU.add).then_inc(r_done, 1)
                    layer_stats(t * 2 - 1)
                if name == "x2":
                    dve.wait_ge(rstd_ready, t * 2 - 1)
                    wait(dve, x2_stored, t * 16 - 16)
                    ts(x2[:], r1[:], mv[:, 0:1], rstd[:], ALU.subtract, ALU.mult).then_inc(x2_done, 1)
                if name == "qk":
                    dve.wait_ge(qk_ps, t)
                    tt(qkT[:], post[:].rearrange("p (m n) -> p m n", m=4), bias_qk[:].unsqueeze(2).broadcast_to([P, 4, P]),
                       ALU.add).then_inc(qk_sb, 1)
                if name == "sc":
                    dve.wait_ge(sc_ps, t)
                    stt(out=sc[:], in0=post[:].rearrange("p (h n) -> p h n", h=MH), scalar=0.125,
                        in1=same_n[:].unsqueeze(1).broadcast_to([P, MH, P]), op0=ALU.mult, op1=ALU.add).then_inc(sc_masked, 1)
                    dve.wait_ge(sc_masked, t)
                    nc.vector.tensor_reduce(nmx[:], sc[:], AX.X, ALU.max, negate=True).then_inc(max_done, 1)
                if name == "pT":
                    dve.wait_ge(exp2_done, t)
                    nc.vector.reciprocal(rden2[:], den2[:]).then_inc(rden2_done, 1)
                if name == "pv2":
                    dve.wait_ge(pv2_ps, t)
                    dve.wait_ge(rden2_done, t)
                    tt(by_head(o2[:]), by_head(post[:, 0:D]), rden2[:].unsqueeze(2).broadcast_to([P, MH, 64]), ALU.mult).then_inc(o2_done, 1)
                if name == "r2":
                    dve.wait_ge(out_ps, t)
                    tt(r1[:], post[:, 0:D], x2[:], ALU.add).then_inc(r_done, 1)
                    layer_stats(t * 2)
                if name == "y1":
                    dve.wait_ge(rstd_ready, t * 2)
                    wait(dve, y1_stored, t * 16 - 16)
                    ts(y1[:], r1[:], mv[:, 0:1], rstd[:], ALU.subtract, ALU.mult).then_inc(y1_norm, 1)
                    dve.wait_ge(y1_norm, t)
                    tt(y1[:], y1[:], gains[:, 0, :], ALU.mult).then_inc(y1_gain, 1)
                    dve.wait_ge(y1_gain, t)
                    tt(y1[:], y1[:], gains[:, 1, :], ALU.add).then_inc(y1_done, 1)
                if name == "gate":
                    dve.wait_ge(gate_ps, t)
                    nc.vector.tensor_reduce(lmax[:], post[:, 0:E], AX.X, ALU.max).then_inc(lmax_done, 1)
                    dve.wait_ge(lmax_done, t)
                    ts(shifted[:], post[:, 0:E], lmax[:], None, ALU.subtract).then_inc(shifted_done, 1)
                    dve.wait_ge(shifted_done, t)
                    stt(out=first[:], in0=shifted[:], scalar=0.0, in1=first_of[:], op0=ALU.is_ge, op1=ALU.mult).then_inc(first_done, 1)
                    dve.wait_ge(first_done, t)
                    nc.vector.tensor_reduce(fmax[:], first[:], AX.X, ALU.max).then_inc(fmax_done, 1)
                if name == "gate_":
                    dve.wait_ge(fmax_done, t)
                    dve.wait_ge(lsum_done, t)
                    nc.vector.reciprocal(lrec[:], lsum[:])
                    at_tile = chosen[:, t - 1, :] if isinstance(t, int) else \
                        chosen[:].rearrange("p t e -> p (t e)")[:, bass.ds((t - 1) * E, E)]
                    ts(at_tile, first[:], fmax[:], None, ALU.is_equal).then_inc(chosen_done, 1)
                    dve.wait_ge(chosen_done, t)
                    ts(gate[:], first[:], fmax[:], lrec[:], ALU.is_equal, ALU.mult).then_inc(gate_done, 1)
                if name in ("moe0", "moe1"):
                    m = int(name[3])
                    if m == 0:
                        dve.wait_ge(gate_done, t)
                        wait(dve, z_stored, t * 16 - 16)
                    for i, bank in enumerate((post, pre)):
                        dve.wait_ge(moe_ps, t * 4 - 4 + (2 * m + i + 1))
                        for e2 in range(2):
                            e = 4 * m + 2 * i + e2
                            src = bank[:, e2 * D:(e2 + 1) * D]
                            if e == 0:
                                ins = ts(z[:], src, gate[:, 0:1], None, ALU.mult)
                            else:
                                dve.wait_ge(z_added, (t - 1) * 8 + e)
                                ins = stt(out=z[:], in0=src, scalar=gate[:, e:e + 1], in1=z[:], op0=ALU.mult, op1=ALU.add)
                            ins.then_inc(z_added, 1)

            prepare("pre_k", -1, 1)
            prepare("pre_q", -1, 1)
            prepare("pre_m", -1, 1)

            def period(t, half, new, old, post_tile, next_half):
                for k in range(NG):
                    if new:
                        product(t, half, k)
                    if k == 1 and old:
                        rows_times_v(*behind(t, half, 0, 1)[:2], NRB - 1)
                    if k in (5, 9) and new:
                        rows_times_v(t, half, (k - 5) // 4)
                    if new if k >= 3 else old:
                        times_v(*behind(t, half, k, 3))
                    if k == 2 and old:
                        reciprocals(t, half)
                    if k == 2 and old:
                        rows_sum(*behind(t, half, 0, 1)[:2], NRB - 1)
                    if k in (6, 10) and new:
                        rows_sum(t, half, (k - 6) // 4)
                    for name in stages("dve", half, k, old, post_tile, next_half):
                        if name == "fin":
                            finish(t, half)
                        prepare(name, t, half)
                        work(name, t)

            all_periods(dve, period)

            done[0] = 0
            def rlink(ins):
                ins.then_inc(rank_seq, 1)
                done[0] += 1
                dve.wait_ge(rank_seq, done[0])

            def by_expert(ap):
                return ap.rearrange("p (t e) -> p e t", e=E)

            restart, count, total, rank = k8[0], kmax, kmin, k8[1]
            rlink(nc.vector.memset(restart[:], 1.0))
            rlink(nc.vector.memset(by_head(restart[:], T)[:, :, 0:1], 0.0))
            dve.wait_ge(rank_ps, 3)
            rlink(nc.vector.tensor_copy(by_head(count[:], T), by_expert(q_ps[1][:])))
            rlink(nc.vector.tensor_tensor_scan(total[:], restart[:], count[:], 0.0, ALU.mult, ALU.add))
            rlink(tt(total[:], total[:], count[:], ALU.subtract))
            rlink(tt(by_head(rank[:], T), by_expert(q_ps[0][:]), by_head(total[:], T), ALU.add))
            rlink(nc.vector.tensor_reduce(first[:], by_expert(v_ps[0][:]), AX.X, ALU.add))
            rlink(tt(by_head(rank[:], T), by_head(rank[:], T), first[:].unsqueeze(2).broadcast_to([P, E, T]), ALU.add))
            rlink(stt(out=by_head(total[:], T), in0=by_head(rank[:], T), scalar=float(CAP),
                      in1=by_expert(chosen[:].rearrange("p t e -> p (t e)")), op0=ALU.is_lt, op1=ALU.mult))
            nc.vector.tensor_reduce(keep[:], total[:].rearrange("p (e t) -> p t e", e=E), AX.X, ALU.add).then_inc(keep_done, 1)
            dve.wait_ge(keep_done, 1)

            PER = 10
            with dve.Fori(0, T // FT // 2) as pair:
                for i in range(2):
                    b = pair * 2 + i
                    buf = last[i]
                    X, Y, Z = (buf[:, :, c, :] for c in range(3))
                    seq = [0]

                    def flink(ins):
                        ins.then_inc(fin_seq, 1)
                        seq[0] += 1
                        dve.wait_ge(fin_seq, b * PER + seq[0])

                    def stats(nth_time):
                        for f in range(FT):
                            ins = nc.vector.bn_stats(st4[:, f, :], Z[:, f, :])
                        flink(ins)
                        nc.vector.memset(var4[:], EPS)
                        for f in range(FT):
                            ins = nc.vector.bn_aggr(mv4[:, f, :], st4[:, f, :])
                        flink(ins)
                        tt(var4[:], mv4[:, :, 1], var4[:], ALU.add).then_inc(fin_var, 1)
                        dve.wait_ge(fin_rstd, b * 2 + nth_time)

                    dve.wait_ge(tiles_loaded[i], pair * 16 + 16)
                    flink(nc.vector.tensor_copy(keep4[i][:], keep[:, bass.ds(b * FT, FT)]))
                    for f in range(FT):
                        ins = stt(out=Z[:, f, :], in0=Z[:, f, :], scalar=keep4[i][:, f:f + 1], in1=Y[:, f, :],
                                  op0=ALU.mult, op1=ALU.add)
                    flink(ins)
                    stats(1)
                    for f in range(FT):
                        ins = ts(Z[:, f, :], Z[:, f, :], mv4[:, f, 0:1], rstd4[:, f:f + 1], ALU.subtract, ALU.mult)
                    flink(ins)
                    flink(tt(Z, Z, gains[:, 2, :].unsqueeze(1).broadcast_to([P, FT, D]), ALU.mult))
                    flink(tt(Z, Z, gains[:, 3, :].unsqueeze(1).broadcast_to([P, FT, D]), ALU.add))
                    flink(tt(Z, Z, X, ALU.add))
                    stats(2)
                    for f in range(FT):
                        ins = ts(X[:, f, :], Z[:, f, :], mv4[:, f, 0:1], rstd4[:, f:f + 1], ALU.subtract, ALU.mult)
                    ins.then_inc(fin_out, 1)


_INS = ["L0_attn_x", "L0_attn_Wq", "L0_attn_bq", "L0_attn_Wk", "L0_attn_bk", "L0_attn_Wv", "L0_attn_bv", "L0_attn_Wo",
        "L0_attn_bo", "L0_ffn_in_proj_w", "L0_ffn_in_proj_b", "L0_ffn_out_proj_w", "L0_ffn_out_proj_b", "L0_ffn_ln1_g",
        "L0_ffn_ln1_b", "L0_ffn_ln2_g", "L0_ffn_ln2_b", "L0_ffn_wg", "L0_ffn_w1", "L0_ffn_b1", "L0_ffn_w2", "L0_ffn_b2"]


def kernel(**inputs):
    import numpy as _np
    import concourse.bacc as _bacc
    from concourse import mybir as _mybir
    from concourse.bass_utils import run_bass_kernel_spmd as _run

    nc = _bacc.Bacc("TRN2", target_bir_lowering=False, num_devices=1)
    arrays, args = {}, []
    for name in _INS:
        a = _np.ascontiguousarray(inputs[name])
        arrays[f"in_{name}_dram"] = a
        args.append(nc.dram_tensor(f"in_{name}_dram", a.shape, _mybir.dt.from_np(a.dtype), kind="ExternalInput").ap())
    args.append(nc.dram_tensor("out_0_dram", (B, S, D), _mybir.dt.float32, kind="ExternalOutput").ap())
    build(nc, *args)
    r = _run(nc, [arrays], core_ids=[0])
    return r.results[0]["out_0_dram"]
```

```python
from contextlib import ExitStack

import concourse.bass as bass
from concourse import mybir

F32 = mybir.dt.float32
BF16 = mybir.dt.bfloat16
ALU = mybir.AluOpType
ACT = mybir.ActivationFunctionType
AX = mybir.AxisListType

P = 128
B, S, D = 8, 1024, 256
NB = P // B
T = S // NB
CH = D // P
H, C = 16, 64
HID = H * C
HH = H // 2
HC = HH * C
MH = 4
E, FF = 8, 1024
FC = FF // P
CAP = B * S // E
EPS = 1e-5
NEG = -1e30

SPLIT = 48
ROWS = C - SPLIT
GROUPS = [g for j in range(0, SPLIT // 2, 4) for g in ((j, 4), (SPLIT - 4 - j, 4))]
NG = len(GROUPS)
SLOTS, VSLOTS = 6, 4
RB = 4
NRB = ROWS // RB
BS = NG // NRB
HALFC = C // 2
POOLED = [(0, 1, 2), (0, 1)]
DIRECT = [(3,), (2,)]
assert NG % SLOTS == 0 and NG % VSLOTS == 0 and NG % NRB == 0 and sum(nj for _, nj in GROUPS) == SPLIT
FT = 2
NBAT, NBUF = T // FT, 8
LAG2 = 3


def size(g):
    j0, nj = GROUPS[g]
    return nj * HH * (SPLIT - j0)


def slot_size(i, slots):
    return max(size(g) for g in range(i, NG, slots))



def build(nc, x, Wq, bq, Wk, bk, Wv, bv, Wo, bo, in_w, in_b, out_w, out_b, g1, be1, g2, be2, wg, w1, b1, w2, b2, out):
    with ExitStack() as ctx:
        def sb(name, shape, dt=F32):
            return ctx.enter_context(nc.sbuf_tensor("sb_" + name, shape, dt))

        def ps(name):
            return ctx.enter_context(nc.psum_tensor("ps_" + name, [P, 512], F32))

        def sems(names):
            return [ctx.enter_context(nc.semaphore(n)) for n in names.split()]

        wqkv = sb("wqkv", [P, CH, 3, HID])
        wo = sb("wo", [P, HID // P, D])
        winT = sb("winT", [P, CH, 3 * D])
        woutT = sb("woutT", [P, CH, D])
        wgate = sb("wgate", [P, CH, E])
        we = sb("we", [P, CH, E * D])
        BO = 3 * HID
        BV, BOUT, BE = BO + D, BO + 2 * D, BO + 3 * D
        NBIAS = BE + E * D
        bias3 = sb("bias3", [3, NBIAS], BF16)
        bias_qk = sb("bias_qk", [P, 4])
        b1T = sb("b1T", [P, FC, E])
        b1c = sb("b1c", [P, FC, 3])
        ones3 = sb("ones3", [3, P], BF16)
        ident = sb("ident", [P, P])
        same_n = sb("same_n", [P, P])
        earlier = sb("earlier", [P, P], BF16)
        entry = sb("entry", [P, P], BF16)
        before = sb("before", [P, P], BF16)
        gains = sb("gains", [P, 4, D])
        scan_max = sb("scan_max", [P, HC])
        scan_min = sb("scan_min", [P, HC])
        first_of = sb("first_of", [P, E])
        NJ = max(nj for _, nj in GROUPS)
        causal = sb("causal", [P, NJ, NJ])
        minus_half = sb("minus_half", [P, 2 * FT])
        minus_later = sb("minus_later", [3, 2])

        x_in = sb("x_in", [P, D])
        xT = sb("xT", [P, CH, P])
        x_res = sb("x_res", [P, D])
        k8 = [sb(f"k8_{i}", [P, HC]) for i in range(2)]
        negm = [sb(f"negm_{i}", [P, HC]) for i in range(2)]
        qrow = [sb(f"qrow_{i}", [P, HH, ROWS]) for i in range(2)]
        kmax = sb("kmax", [P, HC])
        kmin = sb("kmin", [P, HC])
        ARENA = sum(slot_size(i, SLOTS) for i in range(SLOTS)) + sum(slot_size(i, VSLOTS) for i in range(VSLOTS))
        arena = sb("arena", [P, max(ARENA, 5 * 2048)])
        prow = sb("prow", [P, ROWS, HH, C])
        drow = [sb(f"drow_{i}", [P, HH, ROWS]) for i in range(2)]
        dhalf = sb("dhalf", [P, RB, HH, HALFC])
        nrow = sb("nrow", [P, HH, ROWS])
        rden = sb("rden", [P, HH, C])
        attn = sb("attn", [P, HH, C])
        attnT = sb("attnT", [P, HID // P, P])
        r1 = sb("r1", [P, D])
        x2 = sb("x2", [P, D])
        x2T = sb("x2T", [P, CH, P])
        qkT = sb("qkT", [P, 4, P])
        v2 = sb("v2", [P, D])
        sc = sb("sc", [P, MH, P])
        nmx = sb("nmx", [P, MH])
        den2 = sb("den2", [P, MH])
        rden2 = sb("rden2", [P, MH])
        pT = sb("pT", [P, MH, P])
        o2 = sb("o2", [P, D])
        o2T = sb("o2T", [P, CH, P])
        y1 = sb("y1", [P, D])
        y1T = sb("y1T", [P, CH, P])
        shifted, expd, first, gate = [sb(n, [P, E]) for n in ("shifted", "expd", "first", "gate")]
        lmax, lsum, fmax, lrec = [sb(n, [P, 1]) for n in ("lmax", "lsum", "fmax", "lrec")]
        z = sb("z", [P, D])
        st = sb("st", [P, 6])
        mv = sb("mv", [P, 2])
        var = sb("var", [P, 1])
        rstd = sb("rstd", [P, 1])
        chosen = sb("chosen", [P, T, E], BF16)
        keep = sb("keep", [P, T + FT])
        keep_b = [sb(f"keep_b_{i}", [P, FT]) for i in range(2)]
        stats = sb("stats", [P, 2, FT, 6])
        mean_var = [sb(f"mean_var_{i}", [P, 2, FT, 2]) for i in range(2)]
        varf = [sb(f"varf_{i}", [P, 2, FT]) for i in range(2)]
        rstdf = [sb(f"rstdf_{i}", [P, 2, FT]) for i in range(2)]
        shiftf = [sb(f"shiftf_{i}", [P, 2, FT]) for i in range(2)]

        prob, pv, at = [], [], 0
        for i in range(SLOTS):
            prob.append(arena[:, at:at + slot_size(i, SLOTS)])
            at += slot_size(i, SLOTS)
        for i in range(VSLOTS):
            pv.append(arena[:, at:at + slot_size(i, VSLOTS)])
            at += slot_size(i, VSLOTS)
        wide = [arena[:, i * 2048:(i + 1) * 2048] for i in range(5)]
        w1s = [wide[i].rearrange("p (c f) -> p c f", c=CH) for i in range(2)]
        w2s = [wide[2 + i].rearrange("p (c d) -> p c d", c=FC) for i in range(2)]
        w1T = wide[4].rearrange("p (c d) -> p c d", c=FC)
        in_w_raw = wide[0][:, 0:6 * D].rearrange("p (r d) -> p r d", d=D)
        out_w_raw = wide[1][:, 0:2 * D].rearrange("p (r d) -> p r d", d=D)
        b1_raw = wide[2][0:E, 0:FF]
        bqk_raw = wide[3][0:4, 0:P]
        b2_raw = wide[4][0:3, :]
        bias_raw = prow[:].rearrange("p r h c -> p (r h c)")[0:3, 0:NBIAS]
        def batches(ap):
            return [ap[:, i * FT * 3 * D:(i + 1) * FT * 3 * D].rearrange("p (f c d) -> p f c d", f=FT, c=3)
                    for i in range(NBUF // 2)]

        last = batches(wqkv[:].rearrange("p c w n -> p (c w n)")) + batches(arena)

        q_ps = [ps("q0"), ps("q1")]
        v_ps = [ps("v0"), ps("v1")]
        acc_d, acc_n = ps("acc_d"), ps("acc_n")
        post, pre = ps("post"), ps("pre")

        scratch = nc.dram_tensor("scratch", [T, P, 3, D], F32, kind="Internal").ap()

        (consts_ready, loaded_w, loaded_bias, loaded_raw, loaded_gain, loaded_e0, loaded_e1, raw_ps, raw_sb,
         w1T_ps, w1T_sb, b1c_ready, we_ps, we_sb, bias_ready, rows_zero, pool_seq, dve_seq) = sems(
            "consts_ready loaded_w loaded_bias loaded_raw loaded_gain loaded_e0 loaded_e1 raw_ps raw_sb "
            "w1T_ps w1T_sb b1c_ready we_ps we_sb bias_ready rows_zero pool_seq dve_seq")
        (x_loaded, xT_ps, xT_sb, k_ps, k_sb, q_ready, v_ready, kscan, mprod, m_ready, qrow_ready,
         b_done, a_added, a_done, p_done, e_done, d_done, f_done, row_done, rowe_done, rowh_done, rowf_done, dhalf_done, dquarter_done, dsum_done,
         recip_done, finish_done) = sems(
            "x_loaded xT_ps xT_sb k_ps k_sb q_ready v_ready kscan mprod m_ready qrow_ready "
            "b_done a_added a_done p_done e_done d_done f_done row_done rowe_done rowh_done rowf_done dhalf_done dquarter_done dsum_done "
            "recip_done finish_done")
        (at_ps, at_sb, wo_ps, res_loaded, r_done, ln_stats, ln_mean, var_ready, rstd_ready, x2_done, x2_stored,
         x2T_ps, x2T_sb, qk_ps, qk_sb, v2_ps, v2_sb, sc_even, sc_ps, sc_masked, max_done, exp2_done, pT_ps, pT_sb,
         pv2_ps, rden2_done, o2_done, o2T_ps, o2T_sb, out_ps, y1_norm, y1_gain, y1_done, y1_stored, y1T_ps, y1T_sb,
         gate_ps, lmax_done, shifted_done, lsum_done, first_done, fmax_done, chosen_done, gate_done,
         moe_ps, z_added, z_stored) = sems(
            "at_ps at_sb wo_ps res_loaded r_done ln_stats ln_mean var_ready rstd_ready x2_done x2_stored "
            "x2T_ps x2T_sb qk_ps qk_sb v2_ps v2_sb sc_even sc_ps sc_masked max_done exp2_done pT_ps pT_sb "
            "pv2_ps rden2_done o2_done o2T_ps o2T_sb out_ps y1_norm y1_gain y1_done y1_stored y1T_ps y1T_sb "
            "gate_ps lmax_done shifted_done lsum_done first_done fmax_done chosen_done gate_done "
            "moe_ps z_added z_stored")
        (rank_ps, rank_seq, keep_done, keep_copied, fin_seq, fin_var, fin_rstd, fin_shift, fin_norm1, fin_gain, fin_y2, fin_out) = sems(
            "rank_ps rank_seq keep_done keep_copied fin_seq fin_var fin_rstd fin_shift fin_norm1 fin_gain fin_y2 fin_out")
        loaded_e = [loaded_e0, loaded_e1]
        tiles_loaded = [ctx.enter_context(nc.semaphore(f"tiles_loaded{i}")) for i in range(NBUF)]
        out_stored = [ctx.enter_context(nc.semaphore(f"out_stored{i}")) for i in range(NBUF)]

        xt = x.rearrange("l (t n) d -> t l n d", n=NB)
        outt = out.rearrange("l (t n) d -> t l n d", n=NB)

        def tile_of(ap, i):
            if isinstance(i, int):
                return ap[i]
            sub = ap[bass.ds(i, 1)]
            return sub.rearrange("a p c d -> (a p) c d")

        def by_head(ap, w=C):
            return ap.rearrange("p (h c) -> p h c", c=w)

        def group(buf, g):
            j0, nj = GROUPS[g]
            return buf[:, 0:size(g)].rearrange("p (j h i) -> p j h i", j=nj, h=HH)

        def row(ap):
            return ap.rearrange("(a n) -> a n", a=1)

        PLAN = {
            "pe": [{5: ["at", "pre_k"], 6: ["wo"], 7: ["pre_q"], 8: ["x2"], 9: ["qk", "pre_v"], 10: ["v2"], 11: ["sc"]},
                  {1: ["pT"], 2: ["pv2", "pre_x"], 3: ["o2T"], 4: ["out"], 5: ["at", "pre_k"], 6: ["y1T", "pre_q"], 7: ["gate"], 8: ["moe0", "pre_v"], 10: ["moe1"]}],
            "act": [{5: ["at_c"], 7: ["pre_k"], 8: ["x2T_c"], 10: ["v2_c"]},
                   {0: ["exp2"], 1: ["pT_c"], 2: ["pre_x"], 3: ["o2T_c"], 5: ["at_c", "pre_k"], 6: ["y1T_c"], 7: ["gate"]}],
            "dve": [{4: ["fin"], 6: ["r"], 7: ["x2", "pre_k"], 8: ["pre_q"], 9: ["qk", "pre_m"], 11: ["sc"]},
                   {1: ["pT"], 2: ["pv2"], 4: ["fin", "r2"], 5: ["y1"], 6: ["pre_k"], 7: ["gate", "pre_q"], 8: ["gate_", "pre_m"], 9: ["moe0"], 11: ["moe1"]}],
            "dve_early": [{},
                         {}],
            "pool": [{6: ["r"]},
                    {4: ["r2"]}],
        }

        def stages(eng, half, k, old, post_tile, next_half):
            for name in PLAN[eng][half].get(k, []):
                if next_half if name.startswith("pre") else old if name in ("fin", "at", "at_c") else post_tile:
                    yield name

        def all_periods(eng, period):
            period(0, 0, new=True, old=False, post_tile=False, next_half=True)
            period(0, 1, new=True, old=True, post_tile=False, next_half=True)
            with eng.Fori(1, T - 1) as t:
                period(t, 0, new=True, old=True, post_tile=True, next_half=True)
                period(t, 1, new=True, old=True, post_tile=True, next_half=True)
            period(T - 1, 0, new=True, old=True, post_tile=True, next_half=True)
            period(T - 1, 1, new=True, old=True, post_tile=True, next_half=False)
            period(T, 0, new=False, old=True, post_tile=True, next_half=False)
            period(T, 1, new=False, old=False, post_tile=True, next_half=False)

        LAG_D, LAG_E, LAG_F = 4, 4, 5
        LAG_DHALF, LAG_TIMES, LAG_NHALF, LAG_SUM = 2, 3, 4, 5

        def behind(t, half, k, lag):
            if k >= lag:
                return t, half, k - lag
            return (t, 0, k - lag + NG) if half else (t - 1, 1, k - lag + NG)

        def halves(t, half):
            return t * 2 + half

        def row_work(t, half, k, lag, new, old):
            if (k - lag) % BS != BS - 1 or not (new if k >= lag else old):
                return
            tb, hb, kb = behind(t, half, k, lag)
            yield tb, hb, kb // BS

        def nth_block(t, half, b):
            return halves(t, half) * NRB + (b + 1)

        def count(chosen_blocks, t, half, b):
            n = [len(x) for x in chosen_blocks]
            return t * sum(n) + (half * n[0] + sum(x <= b for x in chosen_blocks[half]))

        def pooled(t, half, b):
            return count(POOLED, t, half, b)

        def summed(t, half, b):
            return count([p + d for p, d in zip(POOLED, DIRECT)], t, half, b)

        def nth(t, half, g):
            return t * (2 * NG) + (half * NG + g + 1)

        def wait(eng, sem, value):
            if not isinstance(value, int) or value > 0:
                eng.wait_ge(sem, value)

        def copy_out(eng, ps_sem, n, dst, src, done):
            eng.wait_ge(ps_sem, n)
            (nc.scalar.copy if eng is nc.scalar else nc.vector.tensor_copy)(dst, src).then_inc(done, 1)

        def copies(eng, name, t, half):
            def as_chunks(buf):
                return buf[:].rearrange("p c n -> p (c n)")
            if name == "at_c":
                c0 = 4 * (1 - half)
                if half == 1:
                    wait(eng, wo_ps, t)
                copy_out(eng, at_ps, halves(t, half), attnT[:, c0:c0 + 4, :].rearrange("p c n -> p (c n)"), post[:], at_sb)
            if name == "x2T_c":
                copy_out(eng, x2T_ps, t, as_chunks(x2T), post[:, 0:D], x2T_sb)
            if name == "v2_c":
                copy_out(eng, v2_ps, t, v2[:], post[:, 0:D], v2_sb)
            if name == "pT_c":
                copy_out(eng, pT_ps, t, as_chunks(pT), post[:], pT_sb)
            if name == "o2T_c":
                copy_out(eng, o2T_ps, t, as_chunks(o2T), post[:, 0:D], o2T_sb)
            if name == "y1T_c":
                copy_out(eng, y1T_ps, t, as_chunks(y1T), post[:, 0:D], y1T_sb)

        def kinds(s):
            lo = 1 if isinstance(s, int) and s >= NBAT else 0
            hi = 1 if isinstance(s, int) and s < LAG2 else 2
            return slice(lo, hi)

        def last_pass(eng, step, end):
            for i in range(NBUF):
                step(i, i)
            with eng.Fori(1, NBAT // NBUF) as turn:
                for i in range(NBUF):
                    step(turn * NBUF + i, i)
            for s in range(NBAT, end):
                step(s, s % NBUF)

        def wait_normalised(eng, s):
            if isinstance(s, int) and s < 0:
                return
            eng.wait_ge(fin_norm1, min(s + 1, NBAT) if isinstance(s, int) else s + 1)
            wait(eng, fin_out, s - LAG2 + 1)

        block = ctx.enter_context(nc.Block())

        @block.sync
        def _(sp):
            for i, w in enumerate((Wq, Wk, Wv)):
                sp.dma_start(wqkv[:, :, i, :], w.rearrange("(c p) n -> p c n", p=P)).then_inc(loaded_w, 16)
            sp.dma_start(x_in[:], xt[0]).then_inc(x_loaded, 16)
            sp.dma_start(in_w_raw, in_w.rearrange("(r p) d -> p r d", p=P)).then_inc(loaded_raw, 16)
            sp.dma_start(out_w_raw, out_w.rearrange("(r p) d -> p r d", p=P)).then_inc(loaded_raw, 16)
            sp.dma_start(b1_raw, b1).then_inc(loaded_raw, 16)
            sp.dma_start(bqk_raw, in_b[0:2 * D].rearrange("(r p) -> r p", p=P)).then_inc(loaded_raw, 16)
            for part in range(3):
                for src, at in ((bq, 0), (bk, HID), (bv, 2 * HID), (bo, BO), (in_b[2 * D:3 * D], BV), (out_b, BOUT)):
                    sp.dma_start(bias_raw[part:part + 1, at:at + src.shape[0]], row(src)).then_inc(loaded_bias, 16)
                sp.dma_start(b2_raw[part:part + 1, :], row(b2.rearrange("e d -> (e d)"))).then_inc(loaded_bias, 16)
            sp.dma_start(wo[:], Wo.rearrange("(c p) n -> p c n", p=P)).then_inc(loaded_w, 16)
            sp.dma_start(wgate[:], wg.rearrange("(c p) e -> p c e", p=P)).then_inc(loaded_w, 16)
            for i, src in enumerate((g1, be1, g2, be2)):
                sp.dma_start(gains[:, i, :], row(src).broadcast_to([P, D])).then_inc(loaded_gain, 16)
            sp.wait_ge(raw_sb, 6)
            for e in range(2):
                sp.dma_start(w1s[e], w1[e].rearrange("(c p) f -> p c f", p=P)).then_inc(loaded_e[e], 16)
                sp.dma_start(w2s[e], w2[e].rearrange("(c p) d -> p c d", p=P)).then_inc(loaded_e[e], 16)
            with sp.Fori(1, E // 2) as pair:
                for i in range(2):
                    e = pair * 2 + i
                    sp.wait_ge(we_ps, pair * 2 + (i - 1))
                    sp.dma_start(w1s[i], tile_of(w1.rearrange("e (c p) f -> e p c f", p=P), e)).then_inc(loaded_e[i], 16)
                    sp.dma_start(w2s[i], tile_of(w2.rearrange("e (c p) d -> e p c d", p=P), e)).then_inc(loaded_e[i], 16)

            def period(t, half, new, old, post_tile, next_half):
                if isinstance(t, int) and t == T and half == 0:
                    sp.wait_ge(v_ready, 2 * T)
                    sp.wait_ge(q_ready, 2 * T)
                    sp.wait_ge(x2_stored, 16 * (T - 1))
                    sp.wait_ge(y1_stored, 16 * (T - 1))
                    sp.wait_ge(z_stored, 16 * (T - 1))
                    for i in range(NBUF // 2):
                        load(i, i)
                if half == 0 and new and next_half and not (isinstance(t, int) and t == T - 1):
                    sp.wait_ge(xT_ps, t + 1)
                    sp.dma_start(x_in[:], tile_of(xt, t + 1)).then_inc(x_loaded, 16)
                if not post_tile:
                    return
                if half == 0:
                    wait(sp, r_done, t * 2 - 2)
                    sp.dma_start(x_res[:], tile_of(xt, t - 1)).then_inc(res_loaded, 16)
                    sp.wait_ge(x2_done, t)
                    sp.dma_start(tile_of(scratch, t - 1)[:, 0, :], x2[:]).then_inc(x2_stored, 16)
                else:
                    sp.wait_ge(y1_done, t)
                    sp.dma_start(tile_of(scratch, t - 1)[:, 1, :], y1[:]).then_inc(y1_stored, 16)
                    sp.wait_ge(z_added, t * 8)
                    sp.dma_start(tile_of(scratch, t - 1)[:, 2, :], z[:]).then_inc(z_stored, 16)

            def load(i, b):
                src = scratch[b * FT:(b + 1) * FT] if isinstance(b, int) else scratch[bass.ds(b * FT, FT)]
                sp.dma_start(last[i].rearrange("p f c d -> p f (c d)"),
                             src.rearrange("t p c d -> p t (c d)")).then_inc(tiles_loaded[i], 16)

            def store(i, b):
                sp.wait_ge(fin_out, b + 1)
                for f in range(FT):
                    sp.dma_start(tile_of(outt, b * FT + f), last[i][:, f, 0, :]).then_inc(out_stored[i], 16)

            all_periods(sp, period)

            sp.wait_ge(x2_stored, 16 * T)
            sp.wait_ge(y1_stored, 16 * T)
            sp.wait_ge(z_stored, 16 * T)
            sp.wait_ge(d_done, 2 * T * NG)
            sp.wait_ge(f_done, 2 * T * NG)
            for i in range(NBUF // 2, NBUF):
                load(i, i)
            for b in range(NBUF):
                store(b, b)
                if b > 0:
                    sp.wait_ge(out_stored[b - 1], 16 * FT)
                    load(b - 1, b - 1 + NBUF)
            with sp.Fori(1, NBAT // NBUF - 1) as turn:
                for i in range(NBUF):
                    if i == 0:
                        store(0, turn * NBUF)
                        sp.wait_ge(out_stored[NBUF - 1], turn * (16 * FT))
                        load(NBUF - 1, turn * NBUF + (NBUF - 1))
                    else:
                        store(i, turn * NBUF + i)
                        sp.wait_ge(out_stored[i - 1], turn * (16 * FT) + 16 * FT)
                        load(i - 1, turn * NBUF + (i - 1 + NBUF))
            for i in range(NBUF):
                store(i, NBAT - NBUF + i)
                if i == 0:
                    sp.wait_ge(out_stored[NBUF - 1], (NBAT // NBUF - 1) * 16 * FT)
                    load(NBUF - 1, NBAT - 1)
            for i in range(NBUF):
                sp.wait_ge(out_stored[i], 16 * FT * (NBAT // NBUF))

        @block.gpsimd
        def _(pool):
            done = [0]

            def link(ins):
                ins.then_inc(pool_seq, 1)
                done[0] += 1
                pool.wait_ge(pool_seq, done[0])

            link(nc.gpsimd.memset(ident[:], 1.0))
            link(nc.gpsimd.affine_select(out=ident[:], in_=ident[:], compare_op=ALU.is_equal, fill=0.0, base=0,
                                         pattern=[[-1, P]], channel_multiplier=1))
            link(nc.gpsimd.memset(same_n[:], NEG))
            for l in range(-(B - 1), B):
                link(nc.gpsimd.affine_select(out=same_n[:], in_=same_n[:], compare_op=ALU.not_equal, fill=0.0,
                                             base=l * NB, pattern=[[-1, P]], channel_multiplier=1))
            blocks = [m[:].rearrange("p (l n) -> p l n", n=NB) for m in (entry, before)]
            link(nc.gpsimd.memset(entry[:], 1.0))
            link(nc.gpsimd.affine_select(out=blocks[0], in_=blocks[0], compare_op=ALU.is_ge, fill=0.0, base=0,
                                         pattern=[[-NB, B], [0, NB]], channel_multiplier=1))
            link(nc.gpsimd.affine_select(out=blocks[0], in_=blocks[0], compare_op=ALU.is_ge, fill=0.0, base=NB - 1,
                                         pattern=[[NB, B], [0, NB]], channel_multiplier=-1))
            link(nc.gpsimd.affine_select(out=earlier[:], in_=entry[:], compare_op=ALU.is_ge, fill=0.0, base=-1,
                                         pattern=[[1, P]], channel_multiplier=-1))
            link(nc.gpsimd.memset(before[:], 1.0))
            link(nc.gpsimd.affine_select(out=blocks[1], in_=blocks[1], compare_op=ALU.is_ge, fill=0.0, base=-1,
                                         pattern=[[NB, B], [0, NB]], channel_multiplier=-1))
            link(nc.gpsimd.memset(minus_later[:], -1.0))
            for part in range(2):
                link(nc.gpsimd.affine_select(out=minus_later[:, part:part + 1], in_=minus_later[:, part:part + 1],
                                             compare_op=ALU.is_ge, fill=0.0, base=-1 - part, pattern=[[0, 1]],
                                             channel_multiplier=1))
            link(nc.gpsimd.memset(minus_half[:], -0.5))
            link(nc.gpsimd.memset(causal[:], 0.0))
            link(nc.gpsimd.affine_select(out=causal[:], in_=causal[:], compare_op=ALU.is_ge, fill=NEG, base=0,
                                         pattern=[[-1, NJ], [1, NJ]], channel_multiplier=0))
            nc.gpsimd.memset(ones3[:], 1.0).then_inc(consts_ready, 1)
            pool.wait_ge(bias_ready, 2)
            nc.gpsimd.memset(prow[:], 0.0).then_inc(rows_zero, 1)

            def period(t, half, new, old, post_tile, next_half):
                for k in range(NG):
                    for tb, hb, b in row_work(t, half, k, LAG_DHALF, new, old):
                        if b in POOLED[hb]:
                            n = pooled(tb, hb, b)
                            rows = prow[:, b * RB:(b + 1) * RB]
                            pool.wait_ge(row_done, nth_block(tb, hb, b))
                            wait(pool, dsum_done, summed(tb, hb, b) - 1)
                            nc.gpsimd.tensor_tensor(dhalf[:], rows[:, :, :, 0:HALFC], rows[:, :, :, HALFC:C], ALU.add).then_inc(dhalf_done, 1)
                            pool.wait_ge(dhalf_done, n)
                            quarter = dhalf[:, :, :, 0:HALFC // 2]
                            nc.gpsimd.tensor_tensor(quarter, quarter, dhalf[:, :, :, HALFC // 2:HALFC], ALU.add).then_inc(dquarter_done, 1)
                    for tb, hb, b in row_work(t, half, k, LAG_NHALF, new, old):
                        w = SPLIT + (b + 1) * RB - HALFC
                        rows = prow[:, b * RB:(b + 1) * RB]
                        pool.wait_ge(rowe_done, nth_block(tb, hb, b))
                        nc.gpsimd.tensor_tensor(rows[:, :, :, 0:w], rows[:, :, :, 0:w], rows[:, :, :, HALFC:HALFC + w],
                                                ALU.add).then_inc(rowh_done, 1)
                    if new:
                        n, (j0, nj) = nth(t, half, k), GROUPS[k]
                        p = group(prob[k % SLOTS], k)
                        if k == 0:
                            pool.wait_ge(m_ready, halves(t, half) + 1)
                        pool.wait_ge(b_done, n)
                        nc.gpsimd.tensor_tensor(
                            p, p, by_head(negm[half][:])[:, :, j0:SPLIT].unsqueeze(1).broadcast_to([P, nj, HH, SPLIT - j0]),
                            ALU.add).then_inc(a_added, 1)
                        pool.wait_ge(a_added, n)
                        corner = p[:, :, :, 0:nj]
                        nc.gpsimd.tensor_tensor(corner, corner, causal[:, 0:nj, 0:nj].unsqueeze(2).broadcast_to([P, nj, HH, nj]),
                                                ALU.add).then_inc(a_done, 1)
                    for name in stages("pool", half, k, old, post_tile, next_half):
                        if name in ("r", "r2"):
                            pool.wait_ge(var_ready, t * 2 - (1 if name == "r" else 0))
                            nc.gpsimd.tensor_tensor(rstd[:], var[:], minus_half[:, 0:1], ALU.pow).then_inc(rstd_ready, 1)

            all_periods(pool, period)

            def step(s, i):
                pool.wait_ge(fin_var, s + 1)
                wait_normalised(pool, s - 2)
                k = kinds(s)
                nc.gpsimd.tensor_tensor(rstdf[i % 2][:, k], varf[i % 2][:, k],
                                        minus_half[:].rearrange("p (k f) -> p k f", k=2)[:, k], ALU.pow).then_inc(fin_rstd, 1)
                if not isinstance(s, int) or 0 < s <= NBAT:
                    z_b = last[(i - 1) % NBUF][:, :, 2, :]
                    pool.wait_ge(fin_norm1, s)
                    nc.gpsimd.tensor_tensor(z_b, z_b, gains[:, 2, :].unsqueeze(1).broadcast_to([P, FT, D]), ALU.mult).then_inc(fin_gain, 1)
                    pool.wait_ge(fin_gain, s)
                    nc.gpsimd.tensor_tensor(z_b, z_b, gains[:, 3, :].unsqueeze(1).broadcast_to([P, FT, D]), ALU.add).then_inc(fin_y2, 1)

            last_pass(pool, step, NBAT + LAG2)

        @block.tensor
        def _(pe):
            mm = nc.tensor.matmul
            banks = q_ps + v_ps + [acc_d, acc_n]
            pe.wait_ge(consts_ready, 1)
            pe.wait_ge(loaded_raw, 64)
            for i in range(4):
                src, r0 = (in_w_raw, 2 * i) if i < 3 else (out_w_raw, 0)
                for r in range(2):
                    for c in range(CH):
                        a = (2 * r + c) * P
                        ins = nc.tensor.transpose(banks[i][:, a:a + P], src[:, r0 + r, c * P:(c + 1) * P], ident[:])
                ins.then_inc(raw_ps, 1)
            for c in range(FC):
                ins = nc.tensor.transpose(banks[4][:, c * E:(c + 1) * E], b1_raw[:, c * P:(c + 1) * P], ident[0:E, 0:E])
            ins.then_inc(raw_ps, 1)
            nc.tensor.transpose(banks[5][:, 0:4], bqk_raw, ident[0:4, 0:4]).then_inc(raw_ps, 1)
            pe.wait_ge(raw_sb, 6)
            with pe.Fori(0, E // 2) as pair:
                e0 = pair * 2
                for i in range(2):
                    pe.wait_ge(loaded_e[i], pair * 32 + 32)
                    for b in range(4):
                        for f in range(2):
                            for c in range(CH):
                                a = (2 * f + c) * P
                                ins = nc.tensor.transpose(banks[b][:, a:a + P],
                                                          w1s[i][:, c, (2 * b + f) * P:(2 * b + f + 1) * P], ident[:])
                        ins.then_inc(w1T_ps, 1)
                    pe.wait_ge(w1T_sb, e0 * 4 + (4 * i + 4))
                    pe.wait_ge(b1c_ready, e0 + (i + 1))
                    for c in range(CH):
                        for f in range(FC):
                            mm([acc_d, acc_n][c][:, 0:D], w1T[:, f, c * P:(c + 1) * P], w2s[i][:, f, :],
                               start=(f == 0), stop=(f == FC - 1))
                    for f in range(FC):
                        ins = mm(post[0:3, 0:D], b1c[:, f, :], w2s[i][:, f, :], start=(f == 0), stop=(f == FC - 1))
                    ins.then_inc(we_ps, 1)
                    pe.wait_ge(we_sb, e0 + (i + 1))

            def bias(bank, at, n):
                mm(bank[:, 0:n], ones3[:], bias3[:, at:at + n], start=True, stop=False)

            def project(bank, half, which):
                bias(bank, which * HID + half * HC, HC)
                for c in range(CH):
                    ins = mm(bank[:], xT[:, c, :], wqkv[:, c, which, half * HC:(half + 1) * HC], start=False, stop=(c == CH - 1))
                return ins

            def prepare(name, t, half):
                tn, hn = (t, 1) if half == 0 else (t + 1, 0)
                n = halves(tn, hn)
                if name == "pre_x":
                    pe.wait_ge(x_loaded, tn * 16 + 16)
                    wait(pe, k_sb, n)
                    for c in range(CH):
                        ins = nc.tensor.transpose(pre[:, c * P:(c + 1) * P], x_in[:, c * P:(c + 1) * P], ident[:])
                    ins.then_inc(xT_ps, 1)
                if name == "pre_k":
                    if hn == 0:
                        pe.wait_ge(xT_sb, tn + 1)
                    else:
                        wait(pe, z_added, t * 8 - 8)
                        wait(pe, k_sb, n)
                    project(pre, hn, 1).then_inc(k_ps, 1)
                if name == "pre_q":
                    wait(pe, qrow_ready, n - 1)
                    wait(pe, b_done, nth(t, half, 0) - 1)
                    wait(pe, m_ready, n - 1)
                    project(q_ps[hn], hn, 0).then_inc(q_ready, 1)
                if name == "pre_v":
                    wait(pe, e_done, nth(t, half, 0) - 1)
                    wait(pe, rowe_done, n * NRB - NRB)
                    project(v_ps[hn], hn, 2).then_inc(v_ready, 1)

            def sums(t, half, g, acc, buf, ready, done):
                pe.wait_ge(ready, nth(t, half, g))
                nj, j0 = GROUPS[g][1], GROUPS[g][0]
                for j in range(nj):
                    ins = mm(by_head(acc[:])[:, :, j0:SPLIT], ident[:], group(buf, g)[:, j], start=(g == 0 and j == 0),
                             stop=(g == NG - 1 and j == nj - 1), skip_group_check=True)
                ins.then_inc(done, 1)

            def denominators(t, half, g):
                if g == 0:
                    wait(pe, recip_done, halves(t, half))
                sums(t, half, g, acc_d, prob[g % SLOTS], p_done, d_done)

            def numerators(t, half, g):
                if g == 0:
                    wait(pe, finish_done, halves(t, half))
                sums(t, half, g, acc_n, pv[g % VSLOTS], e_done, f_done)

            def transposes(bank, src, n, done):
                for c in range(n):
                    ins = nc.tensor.transpose(bank[:, c * P:(c + 1) * P], src(c), ident[:])
                ins.then_inc(done, 1)

            def work(name, t, half):
                if name == "at":
                    pe.wait_ge(finish_done, halves(t, half))
                    if half == 0:
                        wait(pe, z_added, t * 8 - 8)
                    else:
                        wait(pe, r_done, t * 2)
                    transposes(post, lambda c: attn[:].rearrange("p h c -> p (h c)")[:, c * P:(c + 1) * P], 4, at_ps)
                if name == "wo":
                    pe.wait_ge(at_sb, t * 2)
                    bias(post, BO, D)
                    for c in range(HID // P):
                        ins = mm(post[:, 0:D], attnT[:, c, :], wo[:, c, :], start=False, stop=(c == HID // P - 1))
                    ins.then_inc(wo_ps, 1)
                if name == "x2":
                    pe.wait_ge(x2_done, t)
                    transposes(post, lambda c: x2[:, c * P:(c + 1) * P], CH, x2T_ps)
                if name == "qk":
                    pe.wait_ge(x2T_sb, t)
                    for m in range(4):
                        for c in range(CH):
                            ins = mm(post[:, m * P:(m + 1) * P], winT[:, c, m * P:(m + 1) * P], x2T[:, c, :],
                                     start=(c == 0), stop=(c == CH - 1))
                    ins.then_inc(qk_ps, 1)
                if name == "v2":
                    pe.wait_ge(qk_sb, t)
                    bias(post, BV, D)
                    for c in range(CH):
                        ins = mm(post[:, 0:D], x2T[:, c, :], winT[:, c, 2 * D:3 * D], start=False, stop=(c == CH - 1))
                    ins.then_inc(v2_ps, 1)
                if name == "sc":
                    pe.wait_ge(v2_sb, t)
                    for a in (0, 64):
                        if a:
                            pe.wait_ge(sc_even, t)
                        for m in range(2):
                            h = 2 * m + a // 64
                            ins = mm(post[:, h * P:(h + 1) * P], qkT[a:a + 64, m, :], qkT[a:a + 64, 2 + m, :],
                                     start=True, stop=True)
                        ins.then_inc(sc_ps if a else sc_even, 1)
                if name == "pT":
                    pe.wait_ge(exp2_done, t)
                    transposes(post, lambda h: sc[:, h, :], MH, pT_ps)
                if name == "pv2":
                    pe.wait_ge(pT_sb, t)
                    for h in range(MH):
                        ins = mm(post[:, h * 64:(h + 1) * 64], pT[:, h, :], v2[:, h * 64:(h + 1) * 64], start=True, stop=True)
                    ins.then_inc(pv2_ps, 1)
                if name == "o2T":
                    pe.wait_ge(o2_done, t)
                    transposes(post, lambda c: o2[:, c * P:(c + 1) * P], CH, o2T_ps)
                if name == "out":
                    pe.wait_ge(o2T_sb, t)
                    bias(post, BOUT, D)
                    for c in range(CH):
                        ins = mm(post[:, 0:D], o2T[:, c, :], woutT[:, c, :], start=False, stop=(c == CH - 1))
                    ins.then_inc(out_ps, 1)
                if name == "y1T":
                    pe.wait_ge(y1_done, t)
                    pe.wait_ge(at_sb, 2 * T if isinstance(t, int) and t == T else t * 2 + 1)
                    transposes(post, lambda c: y1[:, c * P:(c + 1) * P], CH, y1T_ps)
                if name == "gate":
                    pe.wait_ge(y1T_sb, t)
                    for c in range(CH):
                        ins = mm(post[:, 0:E], y1T[:, c, :], wgate[:, c, :], start=(c == 0), stop=(c == CH - 1))
                    ins.then_inc(gate_ps, 1)
                if name in ("moe0", "moe1"):
                    m = int(name[3])
                    for i, bank in enumerate((post, pre)):
                        c4 = 2 * m + i
                        if m == 1:
                            pe.wait_ge(z_added, t * 8 - 8 + 2 * (i + 1))
                        elif i == 0:
                            pe.wait_ge(shifted_done, t)
                        else:
                            pe.wait_ge(k_sb, 2 * T if isinstance(t, int) and t >= T - 1 else halves(t, half) + 2)
                        bias(bank, BE + c4 * 512, 512)
                        for c in range(CH):
                            ins = mm(bank[:], y1T[:, c, :], we[:, c, c4 * 512:(c4 + 1) * 512], start=False, stop=(c == CH - 1))
                        ins.then_inc(moe_ps, 1)

            pe.wait_ge(loaded_w, 80)
            pe.wait_ge(bias_ready, 2)
            prepare("pre_x", -1, 1)
            for name in ("pre_k", "pre_q", "pre_v"):
                prepare(name, -1, 1)

            def period(t, half, new, old, post_tile, next_half):
                for k in range(NG):
                    if k == LAG_F - 1 and old:
                        numerators(*behind(t, half, k, LAG_F))
                    if new if k >= LAG_D else old:
                        denominators(*behind(t, half, k, LAG_D))
                    for name in stages("pe", half, k, old, post_tile, next_half):
                        prepare(name, t, half)
                        work(name, t, half)
                    if k != LAG_F - 1 and (new if k >= LAG_F else old):
                        numerators(*behind(t, half, k, LAG_F))

            all_periods(pe, period)

            pe.wait_ge(chosen_done, T)
            pe.wait_ge(m_ready, 2 * T)
            pe.wait_ge(e_done, 2 * T * NG)
            for m, bank in zip((earlier, entry, before), (q_ps[0], q_ps[1], v_ps[0])):
                mm(bank[:], m[:], chosen[:].rearrange("p t e -> p (t e)"), start=True, stop=True).then_inc(rank_ps, 1)

        @block.scalar
        def _(act):
            go = nc.scalar.activation
            banks = q_ps + v_ps + [acc_d, acc_n]
            for i in range(4):
                act.wait_ge(raw_ps, i + 1)
                dst = winT[:, :, 2 * i * P:(2 * i + 2) * P] if i < 3 else woutT[:]
                nc.scalar.copy(dst.rearrange("p c (r n) -> p r c n", n=P),
                               banks[i][:].rearrange("p (r c n) -> p r c n", r=2, c=CH)).then_inc(raw_sb, 1)
            act.wait_ge(raw_ps, 5)
            nc.scalar.copy(b1T[:], banks[4][:, 0:FC * E].rearrange("p (c e) -> p c e", e=E)).then_inc(raw_sb, 1)
            act.wait_ge(raw_ps, 6)
            nc.scalar.copy(bias_qk[:], banks[5][:, 0:4]).then_inc(raw_sb, 1)
            act.wait_ge(raw_sb, 6)
            act.wait_ge(bias_ready, 1)
            with act.Fori(0, E // 2) as pair:
                e0 = pair * 2
                for i in range(2):
                    for b in range(4):
                        act.wait_ge(w1T_ps, e0 * 4 + (4 * i + b + 1))
                        nc.scalar.copy(w1T[:, 2 * b:2 * b + 2, :].rearrange("p f (c n) -> p f c n", n=P),
                                       banks[b][:].rearrange("p (f c n) -> p f c n", f=2, c=CH)).then_inc(w1T_sb, 1)
                    nc.scalar.copy(b1c[:], b1T[:, :, bass.ds(e0 + i, 1)].broadcast_to([P, FC, 3])).then_inc(b1c_ready, 1)
                    act.wait_ge(we_ps, e0 + (i + 1))
                    for c in range(CH):
                        nc.scalar.copy(we[:, c, bass.ds((e0 + i) * D, D)], [acc_d, acc_n][c][:, 0:D])
                    nc.scalar.copy(bias_raw[:, bass.ds((e0 + i) * D + BE, D)], post[0:3, 0:D]).then_inc(we_sb, 1)

            def prepare(name, t, half):
                tn, hn = (t, 1) if half == 0 else (t + 1, 0)
                n = halves(tn, hn)
                if name == "pre_x":
                    copy_out(act, xT_ps, tn + 1, xT[:].rearrange("p c n -> p (c n)"), pre[:, 0:D], xT_sb)
                if name == "pre_k":
                    act.wait_ge(k_ps, n + 1)
                    wait(act, b_done, nth(t, half, 0) - 1)
                    wait(act, kscan, n * 2 - 2)
                    nc.scalar.mul(k8[hn][:], pre[:], 0.125).then_inc(k_sb, 1)

            def work(name, t):
                if name == "exp2":
                    act.wait_ge(max_done, t)
                    for h in range(MH):
                        ins = go(sc[:, h, :], sc[:, h, :], ACT.Exp, bias=nmx[:, h:h + 1], accum_out=den2[:, h:h + 1])
                    ins.then_inc(exp2_done, 1)
                if name == "gate":
                    act.wait_ge(shifted_done, t)
                    go(expd[:], shifted[:], ACT.Exp, accum_out=lsum[:]).then_inc(lsum_done, 1)

            prepare("pre_x", -1, 1)
            prepare("pre_k", -1, 1)
            act.wait_ge(rows_zero, 1)

            def period(t, half, new, old, post_tile, next_half):
                for k in range(NG):
                    if new if k >= 1 else old:
                        te, he, g = behind(t, half, k, 1)
                        act.wait_ge(a_done, nth(te, he, g))
                        p = prob[g % SLOTS]
                        go(p, p, ACT.Exp).then_inc(p_done, 1) if size(g) == p.shape[1] else \
                            go(p[:, 0:size(g)], p[:, 0:size(g)], ACT.Exp).then_inc(p_done, 1)
                    for name in stages("act", half, k, old, post_tile, next_half):
                        copies(act, name, t, half)
                        prepare(name, t, half)
                        work(name, t)
                    if new:
                        n = halves(t, half)
                        b, part = k // BS, k % BS
                        if k == 0:
                            act.wait_ge(k_sb, n + 1)
                            act.wait_ge(qrow_ready, n + 1)
                            act.wait_ge(m_ready, n + 1)
                            wait(act, finish_done, n - 1)
                        if part == 0:
                            wait(act, rowf_done, n * NRB - NRB + (b + 1))
                        for head_row in range(part * RB * HH // BS, (part + 1) * RB * HH // BS):
                            r, h = b * RB + head_row // HH, head_row % HH
                            i = SPLIT + r
                            args = dict(bias=negm[half][:, h * C + i:h * C + i + 1], scale=qrow[half][:, h, r:r + 1])
                            if b not in POOLED[half] + DIRECT[half]:
                                args["accum_out"] = drow[half][:, h, r:r + 1]
                            ins = go(prow[:, r, h, 0:i + 1], k8[half][:, h * C:h * C + i + 1], ACT.Exp, **args)
                        if part == BS - 1:
                            ins.then_inc(row_done, 1)

            all_periods(act, period)

            def step(s, i):
                act.wait_ge(fin_shift, s + 1)
                for kind in range(2)[kinds(s)]:
                    z_b, out_b = last[(i - LAG2 * kind) % NBUF][:, :, 2, :], last[(i - LAG2 * kind) % NBUF][:, :, 2 - 2 * kind, :]
                    for f in range(FT):
                        ins = go(out_b[:, f], z_b[:, f], ACT.Identity, bias=shiftf[i % 2][:, kind, f:f + 1],
                                 scale=rstdf[i % 2][:, kind, f:f + 1])
                    ins.then_inc(fin_out if kind else fin_norm1, 1)

            last_pass(act, step, NBAT + LAG2)

        @block.vector
        def _(dve):
            tt, stt, ts = nc.vector.tensor_tensor, nc.vector.scalar_tensor_tensor, nc.vector.tensor_scalar
            done = [0]

            def link(ins):
                ins.then_inc(dve_seq, 1)
                done[0] += 1
                dve.wait_ge(dve_seq, done[0])

            link(nc.vector.memset(scan_max[:], 0.0))
            link(nc.vector.memset(scan_min[:], 0.0))
            nc.vector.memset(by_head(scan_max[:])[:, :, 0:1], NEG)
            nc.vector.memset(by_head(scan_min[:])[:, :, 0:1], -NEG)
            for e in range(E):
                ins = nc.vector.memset(first_of[:, e:e + 1], float(E - e))
            link(ins)

            def split(a, b):
                link(nc.vector.tensor_copy(bias3[:, a:b], bias_raw[:, a:b]))
                for part in range(2):
                    link(stt(out=bias_raw[:, a:b], in0=bias3[:, a:b], scalar=minus_later[:, part:part + 1], in1=bias_raw[:, a:b],
                             op0=ALU.mult, op1=ALU.add))
                    ins = nc.vector.tensor_copy(bias3[:, a:b], bias_raw[:, a:b])
                    if part == 0:
                        link(ins)
                return ins

            dve.wait_ge(consts_ready, 1)
            dve.wait_ge(loaded_bias, 3 * 7 * 16)
            keep_b2 = [k8[0], k8[1], kmax, kmin]
            for i, buf in enumerate(keep_b2):
                nc.vector.tensor_copy(buf[0:3, :], b2_raw[:, i * 512:(i + 1) * 512])
            split(0, BE).then_inc(bias_ready, 1)
            dve.wait_ge(bias_ready, 1)
            dve.wait_ge(we_sb, E)
            for i, buf in enumerate(keep_b2):
                part = bias_raw[:, BE + i * 512:BE + (i + 1) * 512]
                ins = tt(part, part, buf[0:3, :], ALU.add)
            link(ins)
            split(BE, NBIAS).then_inc(bias_ready, 1)
            dve.wait_ge(loaded_gain, 64)

            def prepare(name, t, half):
                tn, hn = (t, 1) if half == 0 else (t + 1, 0)
                n = halves(tn, hn)
                if name == "pre_k":
                    dve.wait_ge(k_sb, n + 1)
                    nc.vector.tensor_tensor_scan(kmax[:], scan_max[:], k8[hn][:], 0.0, ALU.add, ALU.max).then_inc(kscan, 1)
                    nc.vector.tensor_tensor_scan(kmin[:], scan_min[:], k8[hn][:], 0.0, ALU.add, ALU.min).then_inc(kscan, 1)
                if name == "pre_q":
                    dve.wait_ge(q_ready, n + 1)
                    wait(dve, row_done, n * NRB - NRB)
                    nc.vector.tensor_copy(qrow[hn][:], by_head(q_ps[hn][:])[:, :, SPLIT:C]).then_inc(qrow_ready, 1)
                    dve.wait_ge(kscan, n * 2 + 2)
                    for buf in (kmax, kmin):
                        stt(out=buf[:], in0=q_ps[hn][:], scalar=-1.0, in1=buf[:], op0=ALU.mult, op1=ALU.mult).then_inc(mprod, 1)
                if name == "pre_m":
                    dve.wait_ge(mprod, n * 2 + 2)
                    wait(dve, a_added, nth(t, half, 0) - 1)
                    tt(negm[hn][:], kmax[:], kmin[:], ALU.min).then_inc(m_ready, 1)

            def product(t, half, g):
                (j0, nj), n = GROUPS[g], nth(t, half, g)
                w = SPLIT - j0
                if g == 0:
                    dve.wait_ge(q_ready, halves(t, half) + 1)
                    dve.wait_ge(k_sb, halves(t, half) + 1)
                wait(dve, d_done, n - SLOTS)
                wait(dve, e_done, n - SLOTS)
                tt(group(prob[g % SLOTS], g),
                   by_head(q_ps[half][:])[:, :, j0:SPLIT].unsqueeze(1).broadcast_to([P, nj, HH, w]),
                   by_head(k8[half][:])[:, :, j0:j0 + nj].rearrange("p h j -> p j h").unsqueeze(3).broadcast_to([P, nj, HH, w]),
                   ALU.mult).then_inc(b_done, 1)

            def times_v(t, half, g):
                (j0, nj), n = GROUPS[g], nth(t, half, g)
                w = SPLIT - j0
                if g == 0:
                    dve.wait_ge(v_ready, halves(t, half) + 1)
                dve.wait_ge(p_done, n)
                wait(dve, f_done, n - VSLOTS)
                tt(group(pv[g % VSLOTS], g), group(prob[g % SLOTS], g),
                   by_head(v_ps[half][:])[:, :, j0:j0 + nj].rearrange("p h j -> p j h").unsqueeze(3).broadcast_to([P, nj, HH, w]),
                   ALU.mult).then_inc(e_done, 1)

            def of_block(buf, b):
                return buf[:, :, b * RB:(b + 1) * RB].rearrange("p h r -> p r h")

            def rows_times_v(t, half, b):
                dve.wait_ge(v_ready, halves(t, half) + 1)
                dve.wait_ge(row_done, nth_block(t, half, b))
                if b in POOLED[half]:
                    dve.wait_ge(dhalf_done, pooled(t, half, b))
                w = SPLIT + (b + 1) * RB
                p = prow[:, b * RB:(b + 1) * RB, :, 0:w]
                if b in DIRECT[half]:
                    nc.vector.tensor_reduce(of_block(drow[half], b), p, AX.X, ALU.add).then_inc(dsum_done, 1)
                    dve.wait_ge(dsum_done, summed(t, half, b))
                tt(p, p, by_head(v_ps[half][:])[:, :, 0:w].unsqueeze(1).broadcast_to([P, RB, HH, w]), ALU.mult).then_inc(rowe_done, 1)

            def rows_sum(t, half, b):
                if b in POOLED[half]:
                    dve.wait_ge(dquarter_done, pooled(t, half, b))
                    nc.vector.tensor_reduce(of_block(drow[half], b), dhalf[:, :, :, 0:HALFC // 2], AX.X, ALU.add).then_inc(dsum_done, 1)
                dve.wait_ge(rowh_done, nth_block(t, half, b))
                nc.vector.tensor_reduce(of_block(nrow, b), prow[:, b * RB:(b + 1) * RB, :, 0:HALFC], AX.X, ALU.add).then_inc(rowf_done, 1)

            def reciprocals(t, half):
                n = halves(t, half)
                other = 1 - half
                dve.wait_ge(d_done, n * NG)
                dve.wait_ge(row_done, n * NRB)
                dve.wait_ge(dsum_done, summed(*behind(t, half, 0, 1)[:2], NRB - 1))
                nc.vector.reciprocal(rden[:, :, 0:SPLIT], by_head(acc_d[:])[:, :, 0:SPLIT])
                nc.vector.reciprocal(rden[:, :, SPLIT:C], drow[other][:]).then_inc(recip_done, 1)

            def finish(t, half):
                n = halves(t, half)
                dve.wait_ge(recip_done, n)
                dve.wait_ge(f_done, n * NG)
                dve.wait_ge(rowf_done, n * NRB)
                wait(dve, at_ps, n - 1)
                tt(attn[:, :, 0:SPLIT], by_head(acc_n[:])[:, :, 0:SPLIT], rden[:, :, 0:SPLIT], ALU.mult)
                tt(attn[:, :, SPLIT:C], nrow[:], rden[:, :, SPLIT:C], ALU.mult).then_inc(finish_done, 1)

            def layer_stats(n):
                dve.wait_ge(r_done, n)
                nc.vector.bn_stats(st[:], r1[:]).then_inc(ln_stats, 1)
                dve.wait_ge(ln_stats, n)
                nc.vector.memset(var[:], EPS)
                nc.vector.bn_aggr(mv[:], st[:]).then_inc(ln_mean, 1)
                dve.wait_ge(ln_mean, n)
                tt(var[:], mv[:, 1:2], var[:], ALU.add).then_inc(var_ready, 1)

            def work(name, t):
                if name == "r":
                    dve.wait_ge(wo_ps, t)
                    dve.wait_ge(res_loaded, t * 16)
                    tt(r1[:], post[:, 0:D], x_res[:], ALU.add).then_inc(r_done, 1)
                    layer_stats(t * 2 - 1)
                if name == "x2":
                    dve.wait_ge(rstd_ready, t * 2 - 1)
                    wait(dve, x2_stored, t * 16 - 16)
                    ts(x2[:], r1[:], mv[:, 0:1], rstd[:], ALU.subtract, ALU.mult).then_inc(x2_done, 1)
                if name == "qk":
                    dve.wait_ge(qk_ps, t)
                    tt(qkT[:], post[:].rearrange("p (m n) -> p m n", m=4), bias_qk[:].unsqueeze(2).broadcast_to([P, 4, P]),
                       ALU.add).then_inc(qk_sb, 1)
                if name == "sc":
                    dve.wait_ge(sc_ps, t)
                    stt(out=sc[:], in0=post[:].rearrange("p (h n) -> p h n", h=MH), scalar=0.125,
                        in1=same_n[:].unsqueeze(1).broadcast_to([P, MH, P]), op0=ALU.mult, op1=ALU.add).then_inc(sc_masked, 1)
                    dve.wait_ge(sc_masked, t)
                    nc.vector.tensor_reduce(nmx[:], sc[:], AX.X, ALU.max, negate=True).then_inc(max_done, 1)
                if name == "pT":
                    dve.wait_ge(exp2_done, t)
                    nc.vector.reciprocal(rden2[:], den2[:]).then_inc(rden2_done, 1)
                if name == "pv2":
                    dve.wait_ge(pv2_ps, t)
                    dve.wait_ge(rden2_done, t)
                    tt(by_head(o2[:]), by_head(post[:, 0:D]), rden2[:].unsqueeze(2).broadcast_to([P, MH, 64]), ALU.mult).then_inc(o2_done, 1)
                if name == "r2":
                    dve.wait_ge(out_ps, t)
                    tt(r1[:], post[:, 0:D], x2[:], ALU.add).then_inc(r_done, 1)
                    layer_stats(t * 2)
                if name == "y1":
                    dve.wait_ge(rstd_ready, t * 2)
                    wait(dve, y1_stored, t * 16 - 16)
                    ts(y1[:], r1[:], mv[:, 0:1], rstd[:], ALU.subtract, ALU.mult).then_inc(y1_norm, 1)
                    dve.wait_ge(y1_norm, t)
                    tt(y1[:], y1[:], gains[:, 0, :], ALU.mult).then_inc(y1_gain, 1)
                    dve.wait_ge(y1_gain, t)
                    tt(y1[:], y1[:], gains[:, 1, :], ALU.add).then_inc(y1_done, 1)
                if name == "gate":
                    dve.wait_ge(gate_ps, t)
                    nc.vector.tensor_reduce(lmax[:], post[:, 0:E], AX.X, ALU.max).then_inc(lmax_done, 1)
                    dve.wait_ge(lmax_done, t)
                    ts(shifted[:], post[:, 0:E], lmax[:], None, ALU.subtract).then_inc(shifted_done, 1)
                    dve.wait_ge(shifted_done, t)
                    stt(out=first[:], in0=shifted[:], scalar=0.0, in1=first_of[:], op0=ALU.is_ge, op1=ALU.mult).then_inc(first_done, 1)
                    dve.wait_ge(first_done, t)
                    nc.vector.tensor_reduce(fmax[:], first[:], AX.X, ALU.max).then_inc(fmax_done, 1)
                if name == "gate_":
                    dve.wait_ge(fmax_done, t)
                    dve.wait_ge(lsum_done, t)
                    nc.vector.reciprocal(lrec[:], lsum[:])
                    at_tile = chosen[:, t - 1, :] if isinstance(t, int) else \
                        chosen[:].rearrange("p t e -> p (t e)")[:, bass.ds((t - 1) * E, E)]
                    ts(at_tile, first[:], fmax[:], None, ALU.is_equal).then_inc(chosen_done, 1)
                    dve.wait_ge(chosen_done, t)
                    ts(gate[:], first[:], fmax[:], lrec[:], ALU.is_equal, ALU.mult).then_inc(gate_done, 1)
                if name in ("moe0", "moe1"):
                    m = int(name[3])
                    if m == 0:
                        dve.wait_ge(gate_done, t)
                        wait(dve, z_stored, t * 16 - 16)
                    for i, bank in enumerate((post, pre)):
                        dve.wait_ge(moe_ps, t * 4 - 4 + (2 * m + i + 1))
                        for e2 in range(2):
                            e = 4 * m + 2 * i + e2
                            src = bank[:, e2 * D:(e2 + 1) * D]
                            if e == 0:
                                ins = ts(z[:], src, gate[:, 0:1], None, ALU.mult)
                            else:
                                dve.wait_ge(z_added, (t - 1) * 8 + e)
                                ins = stt(out=z[:], in0=src, scalar=gate[:, e:e + 1], in1=z[:], op0=ALU.mult, op1=ALU.add)
                            ins.then_inc(z_added, 1)

            prepare("pre_k", -1, 1)
            prepare("pre_q", -1, 1)
            prepare("pre_m", -1, 1)

            def run_stages(plan, t, half, k, old, post_tile, next_half):
                for name in stages(plan, half, k, old, post_tile, next_half):
                    if name == "fin":
                        finish(t, half)
                    copies(dve, name, t, half)
                    prepare(name, t, half)
                    work(name, t)

            def period(t, half, new, old, post_tile, next_half):
                for k in range(NG):
                    if new:
                        product(t, half, k)
                    for block in row_work(t, half, k, LAG_TIMES, new, old):
                        rows_times_v(*block)
                    for block in row_work(t, half, k, LAG_SUM, new, old):
                        rows_sum(*block)
                    run_stages("dve_early", t, half, k, old, post_tile, next_half)
                    if new if k >= LAG_E else old:
                        times_v(*behind(t, half, k, LAG_E))
                    if k == LAG_D - 1 and old:
                        reciprocals(t, half)
                    run_stages("dve", t, half, k, old, post_tile, next_half)

            all_periods(dve, period)

            done[0] = 0
            def rlink(ins):
                ins.then_inc(rank_seq, 1)
                done[0] += 1
                dve.wait_ge(rank_seq, done[0])

            def by_expert(ap):
                return ap.rearrange("p (t e) -> p e t", e=E)

            restart, count, total, rank = k8[0], kmax, kmin, k8[1]
            rlink(nc.vector.memset(restart[:], 1.0))
            rlink(nc.vector.memset(by_head(restart[:], T)[:, :, 0:1], 0.0))
            dve.wait_ge(rank_ps, 3)
            rlink(nc.vector.tensor_copy(by_head(count[:], T), by_expert(q_ps[1][:])))
            rlink(nc.vector.tensor_tensor_scan(total[:], restart[:], count[:], 0.0, ALU.mult, ALU.add))
            rlink(tt(total[:], total[:], count[:], ALU.subtract))
            rlink(tt(by_head(rank[:], T), by_expert(q_ps[0][:]), by_head(total[:], T), ALU.add))
            rlink(nc.vector.tensor_reduce(first[:], by_expert(v_ps[0][:]), AX.X, ALU.add))
            rlink(tt(by_head(rank[:], T), by_head(rank[:], T), first[:].unsqueeze(2).broadcast_to([P, E, T]), ALU.add))
            rlink(stt(out=by_head(total[:], T), in0=by_head(rank[:], T), scalar=float(CAP),
                      in1=by_expert(chosen[:].rearrange("p t e -> p (t e)")), op0=ALU.is_lt, op1=ALU.mult))
            nc.vector.memset(keep[:, T:], 0.0)
            nc.vector.tensor_reduce(keep[:, 0:T], total[:].rearrange("p (e t) -> p t e", e=E), AX.X, ALU.add).then_inc(keep_done, 1)
            dve.wait_ge(keep_done, 1)

            LINKS = 3

            def keep_of(s, i):
                nc.vector.tensor_copy(keep_b[i % 2][:], keep[:, s * FT:(s + 1) * FT] if isinstance(s, int) else
                                      keep[:, bass.ds(s * FT, FT)]).then_inc(keep_copied, 1)

            def step(s, i):
                k = kinds(s)
                seq = [1]

                def flink(ins):
                    ins.then_inc(fin_seq, 1)
                    seq[0] += 1
                    dve.wait_ge(fin_seq, s * LINKS + seq[0])

                if k.start == 0:
                    dve.wait_ge(keep_copied, s + 1)
                    dve.wait_ge(tiles_loaded[i], 16 if isinstance(s, int) else (s - i) * (16 // NBUF) + 16)
                    for f in range(FT):
                        ins = stt(out=last[i][:, f, 2, :], in0=last[i][:, f, 2, :], scalar=keep_b[i % 2][:, f:f + 1],
                                  in1=last[i][:, f, 1, :], op0=ALU.mult, op1=ALU.add)
                if k.stop == 2 and not (isinstance(s, int) and s == NBAT + LAG2):
                    dve.wait_ge(fin_y2, s - LAG2 + 1)
                    before = last[(i - LAG2) % NBUF]
                    ins = tt(before[:, :, 2, :], before[:, :, 2, :], before[:, :, 0, :], ALU.add)
                if not (isinstance(s, int) and s == NBAT + LAG2):
                    ins.then_inc(fin_seq, 1)
                if not isinstance(s, int) or s > 0:
                    j, kb = (i - 1) % 2, kinds(s - 1)
                    dve.wait_ge(fin_rstd, s)
                    wait_normalised(dve, s - 3)
                    stt(out=shiftf[j][:, kb], in0=mean_var[j][:, kb, :, 0], scalar=-1.0, in1=rstdf[j][:, kb],
                        op0=ALU.mult, op1=ALU.mult).then_inc(fin_shift, 1)
                if isinstance(s, int) and s == NBAT + LAG2:
                    return
                dve.wait_ge(fin_seq, s * LINKS + 1)
                for kind in range(2)[k]:
                    for f in range(FT):
                        ins = nc.vector.bn_stats(stats[:, kind, f, :], last[(i - LAG2 * kind) % NBUF][:, f, 2, :])
                flink(ins)
                nc.vector.memset(varf[i % 2][:], EPS)
                for kind in range(2)[k]:
                    for f in range(FT):
                        ins = nc.vector.bn_aggr(mean_var[i % 2][:, kind, f, :], stats[:, kind, f, :])
                flink(ins)
                tt(varf[i % 2][:, k], mean_var[i % 2][:, k, :, 1], varf[i % 2][:, k], ALU.add).then_inc(fin_var, 1)
                if k.start == 0:
                    keep_of(s + 1, i + 1)

            keep_of(0, 0)
            last_pass(dve, step, NBAT + LAG2 + 1)


_INS = ["L0_attn_x", "L0_attn_Wq", "L0_attn_bq", "L0_attn_Wk", "L0_attn_bk", "L0_attn_Wv", "L0_attn_bv", "L0_attn_Wo",
        "L0_attn_bo", "L0_ffn_in_proj_w", "L0_ffn_in_proj_b", "L0_ffn_out_proj_w", "L0_ffn_out_proj_b", "L0_ffn_ln1_g",
        "L0_ffn_ln1_b", "L0_ffn_ln2_g", "L0_ffn_ln2_b", "L0_ffn_wg", "L0_ffn_w1", "L0_ffn_b1", "L0_ffn_w2", "L0_ffn_b2"]


def kernel(**inputs):
    import numpy as _np
    import concourse.bacc as _bacc
    from concourse import mybir as _mybir
    from concourse.bass_utils import run_bass_kernel_spmd as _run

    nc = _bacc.Bacc("TRN2", target_bir_lowering=False, num_devices=1)
    arrays, args = {}, []
    for name in _INS:
        a = _np.ascontiguousarray(inputs[name])
        arrays[f"in_{name}_dram"] = a
        args.append(nc.dram_tensor(f"in_{name}_dram", a.shape, _mybir.dt.from_np(a.dtype), kind="ExternalInput").ap())
    args.append(nc.dram_tensor("out_0_dram", (B, S, D), _mybir.dt.float32, kind="ExternalOutput").ap())
    build(nc, *args)
    r = _run(nc, [arrays], core_ids=[0])
    return r.results[0]["out_0_dram"]
```
